# Optimizing a Trainium2 kernel written in Bass

```python
import numpy as np
import jax
import jax.numpy as jnp

def _softmax(x, axis=-1):
    return jax.nn.softmax(x, axis=axis)

def _gelu(x):
    return jax.nn.gelu(x, approximate=True)

def _silu(x):
    return jax.nn.silu(x)

def _sigmoid(x):
    return jax.nn.sigmoid(x)

def _layernorm(x, axis=-1, eps=1e-05):
    m = jnp.mean(x, axis=axis, keepdims=True)
    v = jnp.var(x, axis=axis, keepdims=True)
    return (x - m) / jnp.sqrt(v + eps)

def _scatter_add(tgt, idx, src, axis=0):
    return tgt.at[idx].add(src)

def _segment_sum(src, seg, n):
    return jax.ops.segment_sum(src, seg, n)
kernel_name = 'mk_seq_postln_d2_jaxref_r8_ef187b'

def setup_inputs(seed: int=0):
    np.random.seed(seed)
    _w = jnp.asarray

    def _L0_attn_setup():
        import jax, jax.numpy as jnp
        import numpy as np
        B, S, E, H = (4, 256, 128, 16)
        D = E // H

        def _split_heads(x):
            b, s, _ = x.shape
            return x.reshape(b, s, H, D).transpose(0, 2, 1, 3)
        key = jax.random.key(seed)
        ks = jax.random.split(key, 6)
        scale = 1.0 / np.sqrt(E)
        return {'inputs': jax.random.normal(ks[0], (B, S, E), dtype=jnp.float32), 'Wq': jax.random.normal(ks[1], (E, E), dtype=jnp.float32) * scale, 'bq': jnp.zeros((E,), dtype=jnp.float32), 'Wk': jax.random.normal(ks[2], (E, E), dtype=jnp.float32) * scale, 'bk': jnp.zeros((E,), dtype=jnp.float32), 'Wv': jax.random.normal(ks[3], (E, E), dtype=jnp.float32) * scale, 'bv': jnp.zeros((E,), dtype=jnp.float32), 'Wo': jax.random.normal(ks[4], (E, E), dtype=jnp.float32) * scale, 'bo': jnp.zeros((E,), dtype=jnp.float32)}
    _L0_attn_in = _L0_attn_setup()

    def _L0_ffn_setup():
        import jax, jax.numpy as jnp
        import numpy as np
        NUM_HEADS = 16
        TOP_K = 2
        ROPE_BASE = 10000.0
        LN_EPS = 1e-05

        def _rope_sin_cos(S, D, dtype):
            inv_freq = 1.0 / ROPE_BASE ** (jnp.arange(0, D, 2, dtype=jnp.float32) / D)
            freqs = jnp.arange(S, dtype=jnp.float32)[:, None] * inv_freq[None, :]
            sin = jnp.sin(freqs).astype(dtype)[None, :, None, :]
            cos = jnp.cos(freqs).astype(dtype)[None, :, None, :]
            return (sin, cos)

        def _apply_rope(x, sin, cos):
            x1, x2 = (x[..., 0::2], x[..., 1::2])
            r1 = x1 * cos - x2 * sin
            r2 = x1 * sin + x2 * cos
            return jnp.stack([r1, r2], axis=-1).reshape(x.shape)

        def _layer_norm(x, w, b):
            mu = jnp.mean(x, axis=-1, keepdims=True)
            var = jnp.mean(jnp.square(x - mu), axis=-1, keepdims=True)
            return (x - mu) * jax.lax.rsqrt(var + LN_EPS) * w + b
        key = jax.random.key(seed)
        ks = jax.random.split(key, 8)
        B, S, E, NE = (2, 256, 128, 8)
        s = 0.02
        return {'x': jax.random.normal(ks[0], (B, S, E), dtype=jnp.float32), 'in_proj_w': jax.random.normal(ks[1], (3 * E, E), dtype=jnp.float32) * s, 'in_proj_b': jnp.zeros((3 * E,), dtype=jnp.float32), 'out_proj_w': jax.random.normal(ks[2], (E, E), dtype=jnp.float32) * s, 'out_proj_b': jnp.zeros((E,), dtype=jnp.float32), 'gate_w': jax.random.normal(ks[3], (NE, E), dtype=jnp.float32) * s, 'gate_b': jnp.zeros((NE,), dtype=jnp.float32), 'expert_w': jax.random.normal(ks[4], (NE, E, E), dtype=jnp.float32) * s, 'expert_b': jnp.zeros((NE, E), dtype=jnp.float32), 'ln1_w': jnp.ones((E,), dtype=jnp.float32), 'ln1_b': jnp.zeros((E,), dtype=jnp.float32), 'ln2_w': jnp.ones((E,), dtype=jnp.float32), 'ln2_b': jnp.zeros((E,), dtype=jnp.float32)}
    _L0_ffn_in = _L0_ffn_setup()

    def _L1_attn_setup():
        import jax, jax.numpy as jnp
        import numpy as np
        D_MODEL = 128
        D_STATE = 128
        D_CONV = 4
        EXPAND = 2
        HEADDIM = 64
        D_INNER = EXPAND * D_MODEL
        NHEADS = D_INNER // HEADDIM
        NGROUPS = 1
        CONV_DIM = D_INNER + 2 * NGROUPS * D_STATE
        D_IN_PROJ = 2 * D_INNER + 2 * NGROUPS * D_STATE + NHEADS
        INTER = 344
        BATCH, SEQLEN = (1, 256)
        EPS = 1e-06

        def rmsnorm(x, w, eps=EPS):
            return x * jax.lax.rsqrt(jnp.mean(x * x, axis=-1, keepdims=True) + eps) * w

        def mamba2_mixer(u, in_proj_w, conv_w, conv_b, dt_bias, A_log, D, ssm_norm_w, out_proj_w):
            b, l, _ = u.shape
            zxbcdt = jnp.einsum('bld,ed->ble', u, in_proj_w)
            z, xBC, dt = jnp.split(zxbcdt, [D_INNER, D_INNER + CONV_DIM], axis=-1)
            xBC_t = jnp.transpose(xBC, (0, 2, 1))
            conv = jax.lax.conv_general_dilated(xBC_t, conv_w[:, None, :], window_strides=(1,), padding=[(D_CONV - 1, 0)], feature_group_count=CONV_DIM)
            xBC = jax.nn.silu(jnp.transpose(conv, (0, 2, 1)) + conv_b)
            x, Bm, Cm = jnp.split(xBC, [D_INNER, D_INNER + NGROUPS * D_STATE], axis=-1)
            x = x.reshape(b, l, NHEADS, HEADDIM)
            dt = jax.nn.softplus(dt + dt_bias)
            A = -jnp.exp(A_log)
            dA = jnp.exp(dt * A)

            def step(h, inputs):
                dA_t, dt_t, B_t, x_t, C_t = inputs
                dBx = jnp.einsum('bh,bn,bhp->bhpn', dt_t, B_t, x_t)
                h = h * dA_t[:, :, None, None] + dBx
                y = jnp.einsum('bhpn,bn->bhp', h, C_t)
                return (h, y)
            h0 = jnp.zeros((b, NHEADS, HEADDIM, D_STATE), u.dtype)
            tm = lambda a: jnp.moveaxis(a, 1, 0)
            _, ys = jax.lax.scan(step, h0, (tm(dA), tm(dt), tm(Bm), tm(x), tm(Cm)))
            y = jnp.moveaxis(ys, 0, 1) + D[None, None, :, None] * x
            y = y.reshape(b, l, D_INNER)
            y = rmsnorm(y * jax.nn.silu(z), ssm_norm_w)
            return jnp.einsum('ble,de->bld', y, out_proj_w)
        key = jax.random.key(seed)
        ks = jax.random.split(key, 10)
        s = lambda k, shape, scale: jax.random.normal(k, shape, jnp.float32) * scale
        return {'hidden_states': s(ks[0], (BATCH, SEQLEN, D_MODEL), 1.0), 'norm_w': jnp.ones((D_MODEL,), jnp.float32), 'in_proj_w': s(ks[1], (D_IN_PROJ, D_MODEL), 0.02), 'conv_w': s(ks[2], (CONV_DIM, D_CONV), 0.2), 'conv_b': jnp.zeros((CONV_DIM,), jnp.float32), 'dt_bias': s(ks[3], (NHEADS,), 0.5), 'A_log': jnp.log(jnp.linspace(1.0, 16.0, NHEADS, dtype=jnp.float32)), 'D': jnp.ones((NHEADS,), jnp.float32), 'ssm_norm_w': jnp.ones((D_INNER,), jnp.float32), 'out_proj_w': s(ks[4], (D_MODEL, D_INNER), 0.02), 'post_norm_w': jnp.ones((D_MODEL,), jnp.float32), 'gate_w': s(ks[5], (INTER, D_MODEL), 0.02), 'up_w': s(ks[6], (INTER, D_MODEL), 0.02), 'down_w': s(ks[7], (D_MODEL, INTER), 0.02)}
    _L1_attn_in = _L1_attn_setup()

    def _L1_ffn_setup():
        import jax, jax.numpy as jnp
        import numpy as np
        B, S, D = (2, 64, 128)
        E, K, I = (16, 8, 128)
        I_SH = 128
        ROUTE_SCALE = 2.826
        key = jax.random.key(seed)
        ks = jax.random.split(key, 8)
        s = 0.02
        return {'x': jax.random.normal(ks[0], (B, S, D), dtype=jnp.float32), 'gate_w': jax.random.normal(ks[1], (E, D), dtype=jnp.float32) * s, 'expert_bias': jnp.zeros((E,), dtype=jnp.float32), 'w_gate': jax.random.normal(ks[2], (E, I, D), dtype=jnp.float32) * s, 'w_up': jax.random.normal(ks[3], (E, I, D), dtype=jnp.float32) * s, 'w_down': jax.random.normal(ks[4], (E, D, I), dtype=jnp.float32) * s, 'shared_gate_w': jax.random.normal(ks[5], (I_SH, D), dtype=jnp.float32) * s, 'shared_up_w': jax.random.normal(ks[6], (I_SH, D), dtype=jnp.float32) * s, 'shared_down_w': jax.random.normal(ks[7], (D, I_SH), dtype=jnp.float32) * s}
    _L1_ffn_in = _L1_ffn_setup()
    _d = {'L0_attn_inputs': _L0_attn_in['inputs'], 'L0_attn_Wq': _L0_attn_in['Wq'], 'L0_attn_bq': _L0_attn_in['bq'], 'L0_attn_Wk': _L0_attn_in['Wk'], 'L0_attn_bk': _L0_attn_in['bk'], 'L0_attn_Wv': _L0_attn_in['Wv'], 'L0_attn_bv': _L0_attn_in['bv'], 'L0_attn_Wo': _L0_attn_in['Wo'], 'L0_attn_bo': _L0_attn_in['bo'], 'L0_ffn_in_proj_w': _L0_ffn_in['in_proj_w'], 'L0_ffn_in_proj_b': _L0_ffn_in['in_proj_b'], 'L0_ffn_out_proj_w': _L0_ffn_in['out_proj_w'], 'L0_ffn_out_proj_b': _L0_ffn_in['out_proj_b'], 'L0_ffn_gate_w': _L0_ffn_in['gate_w'], 'L0_ffn_gate_b': _L0_ffn_in['gate_b'], 'L0_ffn_expert_w': _L0_ffn_in['expert_w'], 'L0_ffn_expert_b': _L0_ffn_in['expert_b'], 'L0_ffn_ln1_w': _L0_ffn_in['ln1_w'], 'L0_ffn_ln1_b': _L0_ffn_in['ln1_b'], 'L0_ffn_ln2_w': _L0_ffn_in['ln2_w'], 'L0_ffn_ln2_b': _L0_ffn_in['ln2_b'], 'L1_attn_norm_w': _L1_attn_in['norm_w'], 'L1_attn_in_proj_w': _L1_attn_in['in_proj_w'], 'L1_attn_conv_w': _L1_attn_in['conv_w'], 'L1_attn_conv_b': _L1_attn_in['conv_b'], 'L1_attn_dt_bias': _L1_attn_in['dt_bias'], 'L1_attn_A_log': _L1_attn_in['A_log'], 'L1_attn_D': _L1_attn_in['D'], 'L1_attn_ssm_norm_w': _L1_attn_in['ssm_norm_w'], 'L1_attn_out_proj_w': _L1_attn_in['out_proj_w'], 'L1_attn_post_norm_w': _L1_attn_in['post_norm_w'], 'L1_attn_gate_w': _L1_attn_in['gate_w'], 'L1_attn_up_w': _L1_attn_in['up_w'], 'L1_attn_down_w': _L1_attn_in['down_w'], 'L1_ffn_gate_w': _L1_ffn_in['gate_w'], 'L1_ffn_expert_bias': _L1_ffn_in['expert_bias'], 'L1_ffn_w_gate': _L1_ffn_in['w_gate'], 'L1_ffn_w_up': _L1_ffn_in['w_up'], 'L1_ffn_w_down': _L1_ffn_in['w_down'], 'L1_ffn_shared_gate_w': _L1_ffn_in['shared_gate_w'], 'L1_ffn_shared_up_w': _L1_ffn_in['shared_up_w'], 'L1_ffn_shared_down_w': _L1_ffn_in['shared_down_w']}
    _x0 = _d['L0_attn_inputs']
    _d['L0_attn_inputs'] = jax.random.normal(jax.random.fold_in(jax.random.key(seed), 1), (1, 2048, 128), dtype=_x0.dtype)
    del _x0
    return _d

def reference(L0_attn_inputs, L0_attn_Wq, L0_attn_bq, L0_attn_Wk, L0_attn_bk, L0_attn_Wv, L0_attn_bv, L0_attn_Wo, L0_attn_bo, L0_ffn_in_proj_w, L0_ffn_in_proj_b, L0_ffn_out_proj_w, L0_ffn_out_proj_b, L0_ffn_gate_w, L0_ffn_gate_b, L0_ffn_expert_w, L0_ffn_expert_b, L0_ffn_ln1_w, L0_ffn_ln1_b, L0_ffn_ln2_w, L0_ffn_ln2_b, L1_attn_norm_w, L1_attn_in_proj_w, L1_attn_conv_w, L1_attn_conv_b, L1_attn_dt_bias, L1_attn_A_log, L1_attn_D, L1_attn_ssm_norm_w, L1_attn_out_proj_w, L1_attn_post_norm_w, L1_attn_gate_w, L1_attn_up_w, L1_attn_down_w, L1_ffn_gate_w, L1_ffn_expert_bias, L1_ffn_w_gate, L1_ffn_w_up, L1_ffn_w_down, L1_ffn_shared_gate_w, L1_ffn_shared_up_w, L1_ffn_shared_down_w):

    def _L0_attn_ref(inputs, Wq, bq, Wk, bk, Wv, bv, Wo, bo):
        import jax, jax.numpy as jnp
        import numpy as np
        B, S, E, H = (4, 256, 128, 16)
        D = E // H

        def _split_heads(x):
            b, s, _ = x.shape
            return x.reshape(b, s, H, D).transpose(0, 2, 1, 3)
        q = _split_heads(inputs @ Wq + bq)
        k = _split_heads(inputs @ Wk + bk)
        v = _split_heads(inputs @ Wv + bv)
        inv_sqrt_d = jnp.float32(1.0) / jnp.sqrt(jnp.float32(D))
        scores = jnp.einsum('bhqd,bhkd->bhqk', q, k) * inv_sqrt_d
        weights = jax.nn.softmax(scores, axis=-1)
        attn = jnp.einsum('bhqk,bhkd->bhqd', weights, v)
        attn = attn.transpose(0, 2, 1, 3).reshape(inputs.shape[0], -1, E)
        return attn @ Wo + bo

    def _L0_ffn_ref(x, in_proj_w, in_proj_b, out_proj_w, out_proj_b, gate_w, gate_b, expert_w, expert_b, ln1_w, ln1_b, ln2_w, ln2_b):
        import jax, jax.numpy as jnp
        import numpy as np
        NUM_HEADS = 16
        TOP_K = 2
        ROPE_BASE = 10000.0
        LN_EPS = 1e-05

        def _rope_sin_cos(S, D, dtype):
            inv_freq = 1.0 / ROPE_BASE ** (jnp.arange(0, D, 2, dtype=jnp.float32) / D)
            freqs = jnp.arange(S, dtype=jnp.float32)[:, None] * inv_freq[None, :]
            sin = jnp.sin(freqs).astype(dtype)[None, :, None, :]
            cos = jnp.cos(freqs).astype(dtype)[None, :, None, :]
            return (sin, cos)

        def _apply_rope(x, sin, cos):
            x1, x2 = (x[..., 0::2], x[..., 1::2])
            r1 = x1 * cos - x2 * sin
            r2 = x1 * sin + x2 * cos
            return jnp.stack([r1, r2], axis=-1).reshape(x.shape)

        def _layer_norm(x, w, b):
            mu = jnp.mean(x, axis=-1, keepdims=True)
            var = jnp.mean(jnp.square(x - mu), axis=-1, keepdims=True)
            return (x - mu) * jax.lax.rsqrt(var + LN_EPS) * w + b
        B, S, E = x.shape
        H = NUM_HEADS
        D = E // H
        xh = x.reshape(B, S, H, D)
        sin, cos = _rope_sin_cos(S, D, x.dtype)
        q_in = _apply_rope(xh, sin, cos).reshape(B, S, E)
        k_in = q_in
        v_in = x
        Wq, Wk, Wv = jnp.split(in_proj_w, 3, axis=0)
        bq, bk, bv = jnp.split(in_proj_b, 3, axis=0)
        q = (q_in @ Wq.T + bq).reshape(B, S, H, D)
        k = (k_in @ Wk.T + bk).reshape(B, S, H, D)
        v = (v_in @ Wv.T + bv).reshape(B, S, H, D)
        scale = 1.0 / jnp.sqrt(jnp.asarray(D, dtype=x.dtype))
        scores = jnp.einsum('bqhd,bkhd->bhqk', q, k) * scale
        causal = jnp.tril(jnp.ones((S, S), dtype=bool))
        scores = jnp.where(causal[None, None], scores, jnp.asarray(-jnp.inf, dtype=scores.dtype))
        attn = jax.nn.softmax(scores, axis=-1)
        ctx = jnp.einsum('bhqk,bkhd->bqhd', attn, v).reshape(B, S, E)
        attn_out = ctx @ out_proj_w.T + out_proj_b
        x1 = _layer_norm(x + attn_out, ln1_w, ln1_b)
        gates = jax.nn.softmax(x1 @ gate_w.T + gate_b, axis=-1)
        _, top_idx = jax.lax.top_k(gates, TOP_K)
        top_gates = jnp.take_along_axis(gates, top_idx, axis=-1)
        expert_outputs = jnp.einsum('bsd,efd->bsef', x1, expert_w) + expert_b[None, None]
        sel = jnp.take_along_axis(expert_outputs, top_idx[..., None], axis=2)
        moe_out = jnp.sum(sel * top_gates[..., None], axis=2)
        return _layer_norm(x1 + moe_out, ln2_w, ln2_b)

    def _L1_attn_ref(hidden_states, norm_w, in_proj_w, conv_w, conv_b, dt_bias, A_log, D, ssm_norm_w, out_proj_w, post_norm_w, gate_w, up_w, down_w):
        import jax, jax.numpy as jnp
        import numpy as np
        D_MODEL = 128
        D_STATE = 128
        D_CONV = 4
        EXPAND = 2
        HEADDIM = 64
        D_INNER = EXPAND * D_MODEL
        NHEADS = D_INNER // HEADDIM
        NGROUPS = 1
        CONV_DIM = D_INNER + 2 * NGROUPS * D_STATE
        D_IN_PROJ = 2 * D_INNER + 2 * NGROUPS * D_STATE + NHEADS
        INTER = 344
        BATCH, SEQLEN = (1, 256)
        EPS = 1e-06

        def rmsnorm(x, w, eps=EPS):
            return x * jax.lax.rsqrt(jnp.mean(x * x, axis=-1, keepdims=True) + eps) * w

        def mamba2_mixer(u, in_proj_w, conv_w, conv_b, dt_bias, A_log, D, ssm_norm_w, out_proj_w):
            b, l, _ = u.shape
            zxbcdt = jnp.einsum('bld,ed->ble', u, in_proj_w)
            z, xBC, dt = jnp.split(zxbcdt, [D_INNER, D_INNER + CONV_DIM], axis=-1)
            xBC_t = jnp.transpose(xBC, (0, 2, 1))
            conv = jax.lax.conv_general_dilated(xBC_t, conv_w[:, None, :], window_strides=(1,), padding=[(D_CONV - 1, 0)], feature_group_count=CONV_DIM)
            xBC = jax.nn.silu(jnp.transpose(conv, (0, 2, 1)) + conv_b)
            x, Bm, Cm = jnp.split(xBC, [D_INNER, D_INNER + NGROUPS * D_STATE], axis=-1)
            x = x.reshape(b, l, NHEADS, HEADDIM)
            dt = jax.nn.softplus(dt + dt_bias)
            A = -jnp.exp(A_log)
            dA = jnp.exp(dt * A)

            def step(h, inputs):
                dA_t, dt_t, B_t, x_t, C_t = inputs
                dBx = jnp.einsum('bh,bn,bhp->bhpn', dt_t, B_t, x_t)
                h = h * dA_t[:, :, None, None] + dBx
                y = jnp.einsum('bhpn,bn->bhp', h, C_t)
                return (h, y)
            h0 = jnp.zeros((b, NHEADS, HEADDIM, D_STATE), u.dtype)
            tm = lambda a: jnp.moveaxis(a, 1, 0)
            _, ys = jax.lax.scan(step, h0, (tm(dA), tm(dt), tm(Bm), tm(x), tm(Cm)))
            y = jnp.moveaxis(ys, 0, 1) + D[None, None, :, None] * x
            y = y.reshape(b, l, D_INNER)
            y = rmsnorm(y * jax.nn.silu(z), ssm_norm_w)
            return jnp.einsum('ble,de->bld', y, out_proj_w)
        residual = hidden_states
        h = rmsnorm(hidden_states, norm_w)
        h = mamba2_mixer(h, in_proj_w, conv_w, conv_b, dt_bias, A_log, D, ssm_norm_w, out_proj_w)
        h = residual + h
        residual = h
        h = rmsnorm(h, post_norm_w)
        h = jnp.einsum('bli,di->bld', jax.nn.silu(jnp.einsum('bld,id->bli', h, gate_w)) * jnp.einsum('bld,id->bli', h, up_w), down_w)
        return residual + h

    def _L1_ffn_ref(x, gate_w, expert_bias, w_gate, w_up, w_down, shared_gate_w, shared_up_w, shared_down_w):
        import jax, jax.numpy as jnp
        import numpy as np
        B, S, D = (2, 64, 128)
        E, K, I = (16, 8, 128)
        I_SH = 128
        ROUTE_SCALE = 2.826
        gates = jnp.einsum('bsd,ed->bse', x, gate_w)
        scores = jax.nn.sigmoid(gates.astype(jnp.float32))
        sel_scores = scores + expert_bias
        _, inds = jax.lax.top_k(sel_scores, K)
        selected = jnp.take_along_axis(scores, inds, axis=-1)
        selected = selected / selected.sum(axis=-1, keepdims=True)
        selected = selected * ROUTE_SCALE
        onehot = jax.nn.one_hot(inds, E, dtype=selected.dtype)
        combine = jnp.einsum('bske,bsk->bse', onehot, selected)
        hg = jnp.einsum('bsd,eid->bsei', x, w_gate)
        hu = jnp.einsum('bsd,eid->bsei', x, w_up)
        h = jax.nn.silu(hg) * hu
        ye = jnp.einsum('bsei,edi->bsed', h, w_down)
        y = jnp.einsum('bsed,bse->bsd', ye, combine).astype(x.dtype)
        g = jnp.einsum('bsd,id->bsi', x, shared_gate_w)
        u = jnp.einsum('bsd,id->bsi', x, shared_up_w)
        y = y + jnp.einsum('bsi,di->bsd', jax.nn.silu(g) * u, shared_down_w)
        return y
    x = L0_attn_inputs
    x = _layernorm(x + _L0_attn_ref(x, L0_attn_Wq, L0_attn_bq, L0_attn_Wk, L0_attn_bk, L0_attn_Wv, L0_attn_bv, L0_attn_Wo, L0_attn_bo), axis=-1)
    x = _layernorm(x + _L0_ffn_ref(x, L0_ffn_in_proj_w, L0_ffn_in_proj_b, L0_ffn_out_proj_w, L0_ffn_out_proj_b, L0_ffn_gate_w, L0_ffn_gate_b, L0_ffn_expert_w, L0_ffn_expert_b, L0_ffn_ln1_w, L0_ffn_ln1_b, L0_ffn_ln2_w, L0_ffn_ln2_b), axis=-1)
    x = _layernorm(x + _L1_attn_ref(x, L1_attn_norm_w, L1_attn_in_proj_w, L1_attn_conv_w, L1_attn_conv_b, L1_attn_dt_bias, L1_attn_A_log, L1_attn_D, L1_attn_ssm_norm_w, L1_attn_out_proj_w, L1_attn_post_norm_w, L1_attn_gate_w, L1_attn_up_w, L1_attn_down_w), axis=-1)
    x = _layernorm(x + _L1_ffn_ref(x, L1_ffn_gate_w, L1_ffn_expert_bias, L1_ffn_w_gate, L1_ffn_w_up, L1_ffn_w_down, L1_ffn_shared_gate_w, L1_ffn_shared_up_w, L1_ffn_shared_down_w), axis=-1)
    return x

_drawn_inputs = setup_inputs


def setup_inputs(seed=0):
    import zlib

    import numpy as np

    out = dict(_drawn_inputs(seed))
    spreads = {'L0_attn_bq': (0.0, 0.8),
     'L0_attn_bk': (0.0, 0.8),
     'L0_attn_bv': (0.0, 0.1),
     'L0_attn_bo': (0.0, 0.1),
     'L0_ffn_in_proj_b': (0.0, 0.554),
     'L0_ffn_out_proj_b': (0.0, 0.1),
     'L0_ffn_gate_b': (0.0, 0.401),
     'L0_ffn_expert_b': (0.0, 0.739),
     'L0_ffn_ln1_w': (1.0, 0.2),
     'L0_ffn_ln1_b': (0.0, 0.1),
     'L0_ffn_ln2_w': (1.0, 0.2),
     'L0_ffn_ln2_b': (0.0, 0.1),
     'L1_attn_norm_w': (1.0, 0.2),
     'L1_attn_conv_b': (0.0, 0.1),
     'L1_attn_D': (1.0, 0.563),
     'L1_attn_ssm_norm_w': (1.0, 0.2),
     'L1_attn_post_norm_w': (1.0, 0.6),
     'L1_ffn_expert_bias': (0.0, 0.8)}
    factors = {'L0_ffn_in_proj_w': 8.0,
     'L0_ffn_out_proj_w': 4.342,
     'L1_attn_dt_bias': 8.0,
     'L1_attn_A_log': 8.0,
     'L1_attn_gate_w': 8.0,
     'L1_attn_up_w': 8.0,
     'L1_attn_down_w': 8.0,
     'L1_ffn_gate_w': 8.0,
     'L1_ffn_w_gate': 8.0,
     'L1_ffn_w_up': 8.0,
     'L1_ffn_w_down': 8.0,
     'L1_ffn_shared_gate_w': 8.0,
     'L1_ffn_shared_up_w': 8.0,
     'L1_ffn_shared_down_w': 8.0}
    for name, (base, spread) in spreads.items():
        noise = np.random.default_rng([zlib.crc32(name.encode()), seed]).standard_normal(out[name].shape)
        drawn = base * np.exp(spread * noise) if base else spread * noise
        out[name] = jnp.asarray(drawn.astype(out[name].dtype))
    for name, factor in factors.items():
        out[name] = (out[name] * factor).astype(out[name].dtype)
    return out
```

```python
from contextlib import ExitStack

import numpy as np
import concourse.bass as bass
from concourse import mybir

F32 = mybir.dt.float32
BF16 = mybir.dt.bfloat16
ALU = mybir.AluOpType
ACT = mybir.ActivationFunctionType
AX_X = mybir.AxisListType.X

P = 128
S = 2048
E = 128
NT = S // P
NB = S // 512
H = 16
D = E // H
SCALE = float(D) ** -0.5
HG = 4
NG = H // HG
NEG = -1.0e30

PAIRS = [(a, b) for a in range(3) for b in range(3)]
SCORE_ROWS = len(PAIRS) * D
OP_ROWS = 96
SHIFT_ROW = OP_ROWS - 3

NE = 8
DI = 2 * E
NS = 128
MH = 4
HD = DI // MH
CONV = 4
INTER = 344
RE = 16
TOPK = 8
ROUTE_SCALE = 2.826

W_COLS = {}
_at = 0
for _name, _n in (("wq", E), ("wk", E), ("wv", E), ("wo", E),
                  ("fq", E), ("fk", E), ("fv", E), ("fo", E), ("fg", NE), ("fe", NE * E),
                  ("mxbc", DI + 2 * NS), ("mzdt", DI + MH), ("mo", 2 * E), ("mg", INTER), ("mu", INTER),
                  ("md", 3 * E), ("rg", RE)):
    W_COLS[_name] = (_at, _at + _n)
    _at += _n
W_N = _at

X_COLS = {"gate": (0, (RE + 1) * E), "up": ((RE + 1) * E, 2 * (RE + 1) * E),
          "down": (2 * (RE + 1) * E, 3 * (RE + 1) * E)}
X_N = 3 * (RE + 1) * E

C_COLS = {}
_at = 0
for _name, _n in (("bq", 1), ("bk", 1), ("fbq", 1), ("fbk", 1), ("mnorm", 1), ("mconv", 4 * CONV),
                  ("mconvb", 4), ("mssm", 2), ("mpost", 1)):
    C_COLS[_name] = (_at, _at + _n)
    _at += _n
C_N = _at

R_COLS = {}
_at = 0
for _name, _n in (("bv", E), ("bo", E), ("fbv", E), ("fbo", E), ("ln1w", E), ("ln1b", E), ("ln2w", E),
                  ("ln2b", E), ("fgb", NE), ("dtb", MH), ("alog", MH), ("dskip", MH), ("ebias", RE)):
    R_COLS[_name] = (_at, _at + _n)
    _at += _n
R_N = _at

K_COLS = {}
_at = 0
for _name, _n in (("ident", P), ("mask_qk", P), ("mask_kq", P), ("upto", P), ("after", P), ("ones", P),
                  ("rank", NE)):
    K_COLS[_name] = (_at, _at + _n)
    _at += _n
K_N = _at


class Core:

    def __init__(self, nc):
        self.nc, self.sems = nc, []

    def sem(self, name):
        self.sems.append(self.nc.alloc_semaphore(name=name))
        return self.sems[-1]

    def recycle(self):
        self.nc.clear_and_free_semaphores(self.sems)
        self.sems = []
        self.nc.all_engine_barrier()

    def sb(self, ctx, name, shape, dt=F32):
        return ctx.enter_context(self.nc.sbuf_tensor(name, shape, dt))

    def w(self, name, rows=P):
        a, b = W_COLS[name]
        return self.W[0:rows, a:b]

    def c(self, name, i=0):
        a = C_COLS[name][0] + i
        return self.C[:, a:a + 1]

    def r(self, name):
        a, b = R_COLS[name]
        return self.R[:, a:b]

    def k(self, name):
        a, b = K_COLS[name]
        return self.K[:, a:b]


def over_tiles(row, n=NT):
    return row.unsqueeze(1).to_broadcast([P, n, row.shape[1]])


def over_cols(col, w):
    return col.unsqueeze(2).to_broadcast([P, col.shape[1], w])


def load_stage(g, aps):
    nc = g.nc
    loaded = g.sem("inputs_loaded")
    const_ready = g.sem("bf16_constants_ready")
    g.parts_dram = nc.dram_tensor("qk_parts", (2, 3, P, S), BF16, kind="Internal").ap()
    with nc.Block() as block:
        @block.sync
        def _(sp):
            sp.dma_start(g.X[:], aps["x"].rearrange("(t p) e -> p t e", p=P)).then_inc(loaded, 16)
            sp.dma_start(g.K[:], aps["consts"]).then_inc(loaded, 16)
            sp.dma_start(g.C[:], aps["cols"]).then_inc(loaded, 16)
            sp.dma_start(g.R[:], aps["rows"].partition_broadcast(P)).then_inc(loaded, 16)
            sp.dma_start(g.W[:], aps["weights"]).then_inc(loaded, 16)
            sp.wait_ge(loaded, 80)

        @block.gpsimd
        def _(pool):
            pool.memset(g.half[:], -0.5).then_inc(const_ready, 1)

        @block.scalar
        def _(act):
            act.wait_ge(loaded, 80)
            nc.scalar.copy(g.identb[:], g.k("ident")).then_inc(const_ready, 1)
            nc.scalar.copy(g.mask_qk[:], g.k("mask_qk")).then_inc(const_ready, 1)
            nc.scalar.copy(g.mask_kq[:], g.k("mask_kq")).then_inc(const_ready, 1)


def project_stage(g, pre, wq, wk, wv, bq, bk, bv, rope):
    nc = g.nc
    with ExitStack() as ctx:
        XT = g.sb(ctx, pre + "XT", [P, S])
        XR = g.sb(ctx, pre + "XR", [P, NT, E]) if rope else None
        XRT = g.sb(ctx, pre + "XRT", [P, S]) if rope else XT
        SN = g.sb(ctx, pre + "SN", [P, NT, E]) if rope else None
        CS = g.sb(ctx, pre + "CS", [P, NT, E]) if rope else None
        QKF = g.sb(ctx, pre + "QKF", [P, 2, S])
        parts = g.sb(ctx, pre + "parts", [P, 2, 3, S], BF16)
        ps = ctx.enter_context(nc.psum_tensor(pre + "proj_ps", [P, 8, 512], F32))
        trig = g.sem(pre + "rope_tables")
        roped = g.sem(pre + "roped")
        xt_ps, xt_sb = g.sem(pre + "xt_ps"), g.sem(pre + "xt_sb")
        xrt_ps, xrt_sb = g.sem(pre + "xrt_ps"), g.sem(pre + "xrt_sb")
        qk_ps, qk_sb = g.sem(pre + "qk_ps"), g.sem(pre + "qk_sb")
        high, rest = g.sem(pre + "high_parts"), g.sem(pre + "rest_parts")
        v_ps, v_sb = g.sem(pre + "v_ps"), g.sem(pre + "v_sb")
        sent = g.sem(pre + "parts_sent")
        with nc.Block() as block:
            @block.sync
            def _(sp):
                if rope:
                    sp.dma_start(CS[:], g.aps["rope_cos"].rearrange("(t p) e -> p t e", p=P)).then_inc(trig, 16)
                    sp.dma_start(SN[:], g.aps["rope_sin"].rearrange("(t p) e -> p t e", p=P)).then_inc(trig, 16)
                for w in range(2):
                    for c in range(3):
                        if c < 2:
                            sp.wait_ge(high, 2 * w + c + 1)
                        else:
                            sp.wait_ge(rest, 2 * w + 2)
                        sp.dma_start(g.parts_dram[w, c], parts[:, w, c, :]).then_inc(sent, 16)
                sp.wait_ge(sent, 6 * 16)

            @block.tensor
            def _(pe):
                for t in range(NT):
                    pe.transpose(ps[:, t // 4, P * (t % 4):P * (t % 4) + P], g.X[:, t, :],
                                 g.k("ident")).then_inc(xt_ps, 1)
                if rope:
                    pe.wait_ge(roped, 3)
                    for t in range(NT):
                        pe.transpose(ps[:, 4 + t // 4, P * (t % 4):P * (t % 4) + P], XR[:, t, :],
                                     g.k("ident")).then_inc(xrt_ps, 1)
                    pe.wait_ge(xrt_sb, NB)
                pe.wait_ge(xt_sb, NB)
                for w, wt in ((0, wq), (1, wk)):
                    for b in range(NB):
                        pe.matmul(ps[:, 4 * w + b, :], g.w(wt), XRT[:, 512 * b:512 * b + 512],
                                  start=True, stop=True).then_inc(qk_ps, 1)
                pe.wait_ge(qk_sb, 1)
                for t in range(NT):
                    pe.matmul(ps[:, t // 4, P * (t % 4):P * (t % 4) + P], XT[:, P * t:P * t + P],
                              g.w(wv), start=True, stop=True).then_inc(v_ps, 1)

            @block.scalar
            def _(act):
                for b in range(NB):
                    act.wait_ge(xt_ps, 4 * b + 4)
                    nc.scalar.copy(XT[:, 512 * b:512 * b + 512], ps[:, b, :]).then_inc(xt_sb, 1)
                if rope:
                    for b in range(NB):
                        act.wait_ge(xrt_ps, 4 * b + 4)
                        nc.scalar.copy(XRT[:, 512 * b:512 * b + 512], ps[:, 4 + b, :]).then_inc(xrt_sb, 1)
                for w, bias in ((0, bq), (1, bk)):
                    act.wait_ge(qk_ps, NB * (w + 1))
                    nc.scalar.activation(QKF[:, w, :], ps[:, 4 * w:4 * w + 4, :], ACT.Identity,
                                         bias=g.c(bias)).then_inc(qk_sb, 1)
                for w in range(2):
                    act.wait_ge(qk_sb, w + 1)
                    nc.scalar.copy(parts[:, w, 0, :], QKF[:, w, :]).then_inc(high, 1)
                    act.wait_ge(rest, 2 * w + 1)
                    nc.scalar.copy(parts[:, w, 1, :], QKF[:, w, :]).then_inc(high, 1)

            @block.vector
            def _(dve):
                if rope:
                    dve.wait_ge(trig, 32)
                    pair = g.X[:].rearrange("p t (i two) -> p (t i) two", two=2)
                    sw = XR[:].rearrange("p t (i two) -> p (t i) two", two=2)
                    sn = SN[:].rearrange("p t (i two) -> p (t i) two", two=2)
                    dve.tensor_tensor(sw[:, :, 0:1], pair[:, :, 1:2], sn[:, :, 0:1], ALU.mult)
                    dve.tensor_tensor(sw[:, :, 1:2], pair[:, :, 0:1], sn[:, :, 1:2],
                                      ALU.mult).then_inc(roped, 1)
                    dve.tensor_tensor(CS[:], g.X[:], CS[:], ALU.mult).then_inc(roped, 1)
                    dve.wait_ge(roped, 2)
                    dve.tensor_tensor(XR[:], XR[:], CS[:], ALU.add).then_inc(roped, 1)
                for w in range(2):
                    dve.wait_ge(high, 2 * w + 1)
                    dve.tensor_tensor(QKF[:, w, :], QKF[:, w, :], parts[:, w, 0, :],
                                      ALU.subtract).then_inc(rest, 1)
                    dve.wait_ge(high, 2 * w + 2)
                    dve.tensor_tensor(parts[:, w, 2, :], QKF[:, w, :], parts[:, w, 1, :],
                                      ALU.subtract).then_inc(rest, 1)
                dve.wait_ge(v_ps, NT)
                dve.tensor_tensor(g.V[:], ps[:, 0:4, :].rearrange("p b (q e) -> p (b q) e", e=E),
                                  over_tiles(g.r(bv)), ALU.add).then_inc(v_sb, 1)


def attention_stage(g, pre, causal):
    nc = g.nc
    UNITS = 2 * NB
    TURNS = NG // 2
    RING = 3
    PRING = 2 * HG
    AHEAD = 6

    def key_tiles(u):
        return 4 * (u % NB) + 4 if causal else NT

    def item_tiles(u, x):
        return 4 * (u % NB) + x // HG + 1 if causal else NT

    def chunks(u, x):
        n = item_tiles(u, x)
        return [(a, min(n, a + 8)) for a in range(0, n, 8)]

    def maxima(first, last):
        out = [("item", first, x) for x in range(AHEAD if first else 0, 16)] + [("fold", first)]
        out += [("item", last, x) for x in range(2)] + [("turn", first)]
        return out + [("item", last, x) for x in range(2, AHEAD)]

    def slots(work):
        return sum(len(chunks(w[1], w[2])) if w[0] == "item" else w[0] == "turn" for w in work)

    before = maxima(0, 1)
    during = [maxima(u + 1, u + 2) for u in range(UNITS)]
    SLOTS_BEFORE = slots(before)
    SLOTS_TURN = sum(slots(w) for w in during)
    STEPS = sum(key_tiles(u) for u in range(UNITS))
    EXPS = HG * STEPS
    assert SLOTS_TURN % 2 == 0 and STEPS % 2 == 0

    with ExitStack() as ctx:
        QA = [g.sb(ctx, f"{pre}QA{i}", [OP_ROWS, HG, S], BF16) for i in range(2)]
        KA = [g.sb(ctx, f"{pre}KA{i}", [OP_ROWS, HG, S], BF16) for i in range(2)]
        VA = [g.sb(ctx, f"{pre}VA{i}", [P, NT, HG, 32]) for i in range(2)]
        probs = g.sb(ctx, pre + "probs", [P, 2, HG, 512])
        part_max = g.sb(ctx, pre + "part_max", [P, 2, 16, 2])
        neg_max = g.sb(ctx, pre + "neg_max", [P, 2, 16])
        ones = g.sb(ctx, pre + "ones", [3, S], BF16)
        mrest = g.sb(ctx, pre + "mrest", [16, P])
        mrow = g.sb(ctx, pre + "mrow", [16, 2, 3, P], BF16)
        ps1 = ctx.enter_context(nc.psum_tensor(pre + "ps1", [P, 2, 1024], F32))
        ps2 = ctx.enter_context(nc.psum_tensor(pre + "ps2", [P, RING, 512], F32))
        psO = ctx.enter_context(nc.psum_tensor(pre + "psO", [P, 512], F32))
        cleared = g.sem(pre + "pads_cleared")
        ones_in = g.sem(pre + "ones_in")
        ld = [g.sem(f"{pre}operands_in{i}") for i in range(2)]
        v_ready = g.sem(pre + "v_copied")
        loads_started, copies_started = g.sem(pre + "loads_started"), g.sem(pre + "copies_started")
        q_scores, q_read = g.sem(pre + "query_scores"), g.sem(pre + "query_scores_read")
        folded, split = g.sem(pre + "maxima_folded"), g.sem(pre + "maxima_split")
        part_step = g.sem(pre + "part_step")
        m_in = [g.sem(f"{pre}max_rows_in{i}") for i in range(2)]
        k_scores = g.sem(pre + "key_scores")
        exp_done = g.sem(pre + "exp_done")
        pv_done = g.sem(pre + "pv_done")
        ot_done = g.sem(pre + "ot_done")
        NLOAD = 2 * len(PAIRS)
        ROWS_UNIT = 16 * 3 * HG

        def rows_sent(it, u):
            return 16 + ROWS_UNIT * (it * (UNITS // 2) + u // 2 + 1)

        def op_loads(sp, par, group):
            for n, (a, b) in enumerate(PAIRS):
                for dst, w, c in ((QA, 0, a), (KA, 1, b)):
                    src = g.parts_dram[w, c].rearrange("(n j d) t -> n d j t", n=NG, j=HG)
                    one = src[bass.ds(group, 1)].rearrange("o d j t -> (o d) j t")
                    sp.dma_start(dst[par][D * n:D * n + D, :, :], one).then_inc(ld[par], 16)

        with nc.Block() as block:
            @block.gpsimd
            def _(pool):
                for i in range(2):
                    pool.memset(QA[i][64:OP_ROWS, :, :], 0.0).then_inc(cleared, 1)
                    pool.memset(KA[i][64:OP_ROWS, :, :], 0.0).then_inc(cleared, 1)
                pool.wait_ge(cleared, 4)
                pool.memset(ones[:], 1.0).then_inc(cleared, 1)
                pool.wait_ge(cleared, 5)
                for i in range(2):
                    pool.memset(VA[i][:], 0.0).then_inc(cleared, 1)
                pool.wait_ge(cleared, 7)
                for i in range(2):
                    pool.memset(VA[i][:, :, :, D:D + 1], 1.0).then_inc(cleared, 1)
                pool.wait_ge(cleared, 9)

                def copy_v(par, group):
                    src = g.V[:].rearrange("p t (n w) -> p n t w", n=NG)
                    one = src[:, bass.ds(group, 1)].rearrange("p o t (j d) -> p (o t) j d", j=HG)
                    pool.tensor_copy(VA[par][:, :, :, 0:D], one).then_inc(v_ready, 1)

                copy_v(0, 0)
                copy_v(1, 1)
                with pool.Fori(0, TURNS) as it:
                    pool.wait_ge(pv_done, it * STEPS + STEPS // 2 + 2)
                    pool.sem_inc(copies_started, 1)
                    copy_v(0, 2 - 2 * it)
                    pool.wait_ge(pv_done, it * STEPS + STEPS + 2)
                    pool.sem_inc(copies_started, 1)
                    copy_v(1, 3 - 2 * it)

            @block.sync
            def _(sp):
                for i in range(2):
                    sp.nop().then_inc(m_in[i], 16)
                sp.wait_ge(cleared, 5)
                for i in range(2):
                    for j in range(HG):
                        sp.dma_start(KA[i][SHIFT_ROW:OP_ROWS, j, :], ones[:]).then_inc(ones_in, 16)
                op_loads(sp, 0, 0)
                op_loads(sp, 1, 1)

                def send_rows(it, u):
                    par, i = (u // NB) % 2, u % NB
                    sp.wait_ge(split, it * UNITS + u + 1)
                    for c in range(3):
                        for j in range(HG):
                            dst = QA[par][SHIFT_ROW + c:SHIFT_ROW + c + 1, j, 512 * i:512 * i + 512]
                            sp.dma_start(dst.rearrange("o (q t) -> o q t", q=4),
                                         mrow[4 * j:4 * j + 4, u % 2, c, :]).then_inc(m_in[u % 2], 16)

                send_rows(0, 0)
                with sp.Fori(0, TURNS) as it:
                    for u in range(UNITS):
                        if u == NB:
                            sp.wait_ge(pv_done, it * STEPS + STEPS // 2 + 2)
                            sp.sem_inc(loads_started, 1)
                            op_loads(sp, 0, 2 - 2 * it)
                        send_rows(it, u + 1)
                    sp.wait_ge(pv_done, it * STEPS + STEPS + 2)
                    sp.sem_inc(loads_started, 1)
                    op_loads(sp, 1, 3 - 2 * it)
                for i in range(2):
                    sp.wait_ge(ld[i], 16 * NLOAD * (TURNS + 1))
                    sp.wait_ge(m_in[i], rows_sent(TURNS, 0) - ROWS_UNIT * i)
                sp.wait_ge(ones_in, 16 * 2 * HG)

            @block.tensor
            def _(pe):
                def item(it, k, u, x):
                    par, q, j = (u // NB) % 2, x // HG, x % HG
                    qt = 4 * (u % NB) + q
                    if u % NB == 0 and x == 0:
                        pe.wait_ge(ld[par], 16 * NLOAD * (it + 1 + u // UNITS))
                    for a, b in chunks(u, x):
                        buf = k % 2
                        if k >= 2:
                            pe.wait_ge(q_read, it * SLOTS_TURN + k - 1)
                        for c in range(a, b, 4):
                            e = min(b, c + 4)
                            diag = causal and e == qt + 1
                            mm = pe.matmul(ps1[:, buf, P * (c - a):P * (e - a)],
                                           QA[par][0:SHIFT_ROW, j, P * qt:P * qt + P],
                                           KA[par][0:SHIFT_ROW, j, P * c:P * e],
                                           start=True, stop=not diag)
                            if diag:
                                mm = pe.matmul(ps1[:, buf, P * (e - 1 - a):P * (e - a)], g.identb[:],
                                               g.mask_qk[:], start=False, stop=True)
                        mm.then_inc(q_scores, 1)
                        k += 1
                    return k

                def turn(it, k, u):
                    pe.wait_ge(q_read, it * SLOTS_TURN + k - 1)
                    pe.wait_ge(folded, it * UNITS + u + 1)
                    pe.transpose(ps1[0:16, k % 2, 0:P], neg_max[:, u % 2, :], g.k("ident")).then_inc(q_scores, 1)
                    return k + 1

                def maxima_work(it, k, work):
                    for w in work:
                        if w[0] == "item":
                            k = item(it, k, w[1], w[2])
                        elif w[0] == "turn":
                            k = turn(it, k, w[1])
                    return k

                def key_scores(it, u, s, j, n):
                    par, i = (u // NB) % 2, u % NB
                    if n < RING:
                        pe.wait_ge(exp_done, it * EXPS + RING)
                    else:
                        pe.wait_ge(exp_done, it * EXPS + n + 1)
                    lo = max(0, P * (s - 4 * i)) if causal else 0
                    diag = causal and s >= 4 * i
                    mm = pe.matmul(ps2[:, n % RING, lo:512], KA[par][:, j, P * s:P * s + P],
                                   QA[par][:, j, 512 * i + lo:512 * i + 512], start=True, stop=not diag)
                    if diag:
                        mm = pe.matmul(ps2[:, n % RING, lo:lo + P], g.identb[:], g.mask_kq[:],
                                       start=False, stop=True)
                    mm.then_inc(k_scores, 1)

                def sum_step(it, u, s, st):
                    par, i = (u // NB) % 2, u % NB
                    pe.wait_ge(exp_done, it * EXPS + RING + HG * (st + 1))
                    if s == 0:
                        pe.wait_ge(ot_done, it * UNITS + u + 1)
                        if i == 0:
                            pe.wait_ge(v_ready, it * 2 + par + 1)
                    lo = max(0, P * (s - 4 * i)) if causal else 0
                    for j in range(HG):
                        mm = pe.matmul(psO[32 * j:32 * j + 32, lo:512], VA[par][:, s, j, :],
                                       probs[:, st % 2, j, lo:512], start=(s == 0),
                                       stop=(s == key_tiles(u) - 1))
                    mm.then_inc(pv_done, 1)

                pe.nop().then_inc(pv_done, 2)
                pe.wait_ge(cleared, 9)
                pe.wait_ge(ones_in, 16 * 2 * HG)
                maxima_work(0, 0, before)
                with pe.Fori(0, TURNS) as it:
                    st, k = 0, SLOTS_BEFORE
                    last = None
                    for u in range(UNITS):
                        n, done = key_tiles(u), 0
                        for s in range(n):
                            if s == 0:
                                pe.wait_ge(m_in[u % 2], rows_sent(it, u))
                            key_scores(it, u, s, 0, HG * st)
                            key_scores(it, u, s, 1, HG * st + 1)
                            upto = len(during[u]) * (s + 1) // n
                            k = maxima_work(it, k, during[u][done:upto])
                            done = upto
                            key_scores(it, u, s, 2, HG * st + 2)
                            key_scores(it, u, s, 3, HG * st + 3)
                            if last:
                                sum_step(it, *last)
                            last = (u, s, st)
                            st += 1
                    sum_step(it, *last)

            @block.scalar
            def _(act):
                def copy_out(it, u, st):
                    act.wait_ge(pv_done, it * STEPS + st + 2)
                    group = 2 * it + u // NB
                    dst = g.OT[:, bass.ds(group, 1), 512 * (u % NB):512 * (u % NB) + 512]
                    nc.scalar.copy(dst.rearrange("p o t -> p (o t)"), psO[:]).then_inc(ot_done, 1)

                act.nop().then_inc(exp_done, RING)
                act.nop().then_inc(ot_done, 1)
                with act.Fori(0, TURNS) as it:
                    st = 0
                    for u in range(UNITS):
                        for s in range(key_tiles(u)):
                            lo = max(0, P * (s - 4 * (u % NB))) if causal else 0
                            act.wait_ge(pv_done, it * STEPS + st + 1)
                            for j in range(HG):
                                n = HG * st + j
                                act.wait_ge(k_scores, it * EXPS + n + 1)
                                nc.scalar.activation(probs[:, st % 2, j, lo:512], ps2[:, n % RING, lo:512],
                                                     ACT.Exp, scale=SCALE).then_inc(exp_done, 1)
                            if s == 0 and u:
                                copy_out(it, u - 1, st)
                            st += 1
                    copy_out(it, UNITS - 1, st)

            @block.vector
            def _(dve):
                def fold(it, k, u):
                    dve.wait_ge(q_read, it * SLOTS_TURN + k)
                    if len(chunks(u, 0)) == 2:
                        ins = dve.tensor_reduce(neg_max[:, u % 2, :], part_max[:, u % 2, :, :], AX_X,
                                                ALU.max, negate=True)
                    else:
                        ins = dve.tensor_scalar(neg_max[:, u % 2, :], part_max[:, u % 2, :, 0], -1.0, None,
                                                ALU.mult)
                    ins.then_inc(folded, 1)

                def parts(it, k, u):
                    dve.wait_ge(q_scores, it * SLOTS_TURN + k + 1)
                    dve.wait_ge(m_in[u % 2], rows_sent(it, u) - ROWS_UNIT)
                    row = ps1[0:16, k % 2, 0:P]
                    dve.tensor_copy(mrow[:, u % 2, 0, :], row).then_inc(part_step, 1)
                    dve.wait_ge(part_step, 2 * (it * UNITS + u) + 1)
                    dve.tensor_tensor(mrest[:], row, mrow[:, u % 2, 0, :], ALU.subtract).then_inc(q_read, 1)
                    dve.wait_ge(q_read, it * SLOTS_TURN + k + 1)
                    dve.tensor_copy(mrow[:, u % 2, 1, :], mrest[:]).then_inc(part_step, 1)
                    dve.wait_ge(part_step, 2 * (it * UNITS + u) + 2)
                    dve.tensor_tensor(mrow[:, u % 2, 2, :], mrest[:], mrow[:, u % 2, 1, :],
                                      ALU.subtract).then_inc(split, 1)
                    return k + 1

                def maxima_work(it, k, work):
                    for w in work:
                        if w[0] == "fold":
                            fold(it, k, w[1])
                        elif w[0] == "turn":
                            k = parts(it, k, w[1])
                        else:
                            u, x = w[1], w[2]
                            col = 4 * (x % HG) + x // HG
                            for c, (a, b) in enumerate(chunks(u, x)):
                                dve.wait_ge(q_scores, it * SLOTS_TURN + k + 1)
                                dve.tensor_reduce(part_max[:, u % 2, col, c:c + 1],
                                                  ps1[:, k % 2, 0:P * (b - a)], AX_X, ALU.max)\
                                   .then_inc(q_read, 1)
                                k += 1
                    return k

                maxima_work(0, 0, before)
                with dve.Fori(0, TURNS) as it:
                    k = SLOTS_BEFORE
                    for u in range(UNITS):
                        k = maxima_work(it, k, during[u])


def attention_out_stage(g, pre, wo, bo):
    nc = g.nc
    with ExitStack() as ctx:
        A = g.sb(ctx, pre + "A", [P, NT, E])
        AT = g.sb(ctx, pre + "AT", [P, S])
        inv = g.sb(ctx, pre + "inv", [P, NT, H])
        ps = ctx.enter_context(nc.psum_tensor(pre + "out_ps", [P, 8, 512], F32))
        o_ps, inv_done, a_done = g.sem(pre + "o_ps"), g.sem(pre + "inv_done"), g.sem(pre + "a_done")
        at_ps, at_sb = g.sem(pre + "at_ps"), g.sem(pre + "at_sb")
        y_ps, bias_in, y_done = g.sem(pre + "y_ps"), g.sem(pre + "bias_in"), g.sem(pre + "y_done")
        with nc.Block() as block:
            @block.tensor
            def _(pe):
                for t in range(NT):
                    if t >= 8:
                        pe.wait_ge(a_done, (t - 8) // 4 + 1)
                    for n in range(NG):
                        mm = pe.transpose(ps[:, t % 8, P * n:P * n + P], g.OT[:, n, P * t:P * t + P],
                                          g.k("ident"))
                    mm.then_inc(o_ps, 1)
                for t in range(NT):
                    pe.wait_ge(a_done, max(t // 4 + 1, 3 if t < 8 else 4))
                    pe.transpose(ps[:, t // 4, P * (t % 4):P * (t % 4) + P], A[:, t, :],
                                 g.k("ident")).then_inc(at_ps, 1)
                for t in range(NT):
                    pe.wait_ge(at_sb, t // 4 + 1)
                    pe.matmul(ps[:, 4 + t // 4, P * (t % 4):P * (t % 4) + P], AT[:, P * t:P * t + P],
                              g.w(wo), start=True, stop=True).then_inc(y_ps, 1)

            @block.scalar
            def _(act):
                for b in range(NB):
                    act.wait_ge(at_ps, 4 * b + 4)
                    nc.scalar.copy(AT[:, 512 * b:512 * b + 512], ps[:, b, :]).then_inc(at_sb, 1)

            @block.gpsimd
            def _(pool):
                pool.tensor_tensor(g.Y[:], g.X[:], over_tiles(g.r(bo)), ALU.add).then_inc(bias_in, 1)

            @block.vector
            def _(dve):
                for b in range(NB):
                    dve.wait_ge(o_ps, 4 * b + 4)
                    heads = ps[:, 4 * (b % 2):4 * (b % 2) + 4, :].rearrange("p q (h w) -> p (q h) w", w=32)
                    r = inv[:, 4 * b:4 * b + 4, :].rearrange("p q h -> p (q h)")
                    dve.reciprocal(r, heads[:, :, D]).then_inc(inv_done, 1)
                    dve.wait_ge(inv_done, b + 1)
                    dve.tensor_tensor(A[:, 4 * b:4 * b + 4, :].rearrange("p q (h d) -> p (q h) d", d=D),
                                      heads[:, :, 0:D], over_cols(r, D), ALU.mult).then_inc(a_done, 1)
                dve.wait_ge(y_ps, NT)
                dve.wait_ge(bias_in, 1)
                dve.tensor_tensor(g.Y[:], g.Y[:], ps[:, 4:8, :].rearrange("p b (q e) -> p (b q) e", e=E),
                                  ALU.add).then_inc(y_done, 1)


def norm_ops(g, ctx, pre, block, start, start_at, eps, weight=None, bias=None, out=None):
    nc = g.nc
    out = g.X if out is None else out
    sums = g.sb(ctx, pre + "sums", [P, NT])
    sq = g.sb(ctx, pre + "sq", [P, NT, E])
    var = g.sb(ctx, pre + "var", [P, NT])
    mean_done, centred, squared = g.sem(pre + "mean_done"), g.sem(pre + "centred"), g.sem(pre + "squared")
    var_done, rstd_done, normed = g.sem(pre + "var_done"), g.sem(pre + "rstd_done"), g.sem(pre + "normed")
    halves = [(0, NT // 2), (NT // 2, NT)]
    with g.nc.Block() as block:
        @block.vector
        def _(dve):
            for a, b in halves:
                dve.tensor_reduce(sums[:, a:b], g.Y[:, a:b, :], AX_X, ALU.add).then_inc(mean_done, 1)
            for n, (a, b) in enumerate(halves):
                dve.wait_ge(mean_done, n + 1)
                dve.scalar_tensor_tensor(out=g.Y[:, a:b, :], in0=over_cols(sums[:, a:b], E), scalar=-1.0 / E,
                                         in1=g.Y[:, a:b, :], op0=ALU.mult, op1=ALU.add).then_inc(centred, 1)
            for n, (a, b) in enumerate(halves):
                dve.wait_ge(squared, n + 1)
                dve.tensor_reduce(var[:, a:b], sq[:, a:b, :], AX_X, ALU.add).then_inc(var_done, 1)
                dve.wait_ge(var_done, 3 * n + 1)
                dve.tensor_scalar(var[:, a:b], var[:, a:b], 1.0 / E, eps, ALU.mult, ALU.add).then_inc(var_done, 1)
                dve.wait_ge(rstd_done, n + 1)
                dve.tensor_tensor(out[:, a:b, :], g.Y[:, a:b, :], over_cols(var[:, a:b], E),
                                  ALU.mult).then_inc(var_done, 1)
            if weight:
                dve.wait_ge(var_done, 6)
                dve.tensor_tensor(out[:], out[:], over_tiles(g.r(weight)), ALU.mult).then_inc(normed, 1)
                dve.wait_ge(normed, 1)
                dve.tensor_tensor(out[:], out[:], over_tiles(g.r(bias)), ALU.add).then_inc(normed, 1)

        @block.scalar
        def _(act):
            for n, (a, b) in enumerate(halves):
                act.wait_ge(centred, n + 1)
                nc.scalar.activation(sq[:, a:b, :], g.Y[:, a:b, :], ACT.Square).then_inc(squared, 1)

        @block.gpsimd
        def _(pool):
            for n, (a, b) in enumerate(halves):
                pool.wait_ge(var_done, 3 * n + 2)
                pool.tensor_tensor(var[:, a:b], var[:, a:b], g.half[:, a:b], ALU.pow).then_inc(rstd_done, 1)


def norm_stage(g, pre, eps=1e-5, weight=None, bias=None, out=None):
    with ExitStack() as ctx:
        norm_ops(g, ctx, pre, None, None, None, eps, weight, bias, out)


def transpose_ops(g, src, ps, done, wait=None):
    for t in range(NT):
        g.nc.tensor.transpose(ps[:, t // 4, P * (t % 4):P * (t % 4) + P], src[:, t, :],
                              g.k("ident")).then_inc(done, 1)


def experts2_stage(g):
    nc = g.nc
    with ExitStack() as ctx:
        X1T = g.sb(ctx, "e2_X1T", [P, S])
        gates = g.sb(ctx, "e2_gates", [P, NT, NE])
        left = g.sb(ctx, "e2_left", [P, NT, NE])
        mark = g.sb(ctx, "e2_mark", [P, NT, NE])
        pick = g.sb(ctx, "e2_pick", [P, 2, NT, NE])
        best = g.sb(ctx, "e2_best", [P, NT])
        first = g.sb(ctx, "e2_first", [P, NT])
        comb = g.sb(ctx, "e2_comb", [P, NT, NE])
        combT = g.sb(ctx, "e2_combT", [NE, S])
        eb = g.sb(ctx, "e2_eb", [NE, E])
        ps = ctx.enter_context(nc.psum_tensor("e2_ps", [P, 8, 512], F32))
        eb_in = g.sem("e2_bias_in")
        xt_ps, xt_sb, logits = g.sem("e2_xt_ps"), g.sem("e2_xt_sb"), g.sem("e2_logits")
        step, exps = g.sem("e2_dve_step"), g.sem("e2_exp")
        ct_ps, ct_sb, bias_ps = g.sem("e2_ct_ps"), g.sem("e2_ct_sb"), g.sem("e2_bias_ps")
        y_start, e_ps, e_read = g.sem("e2_y_start"), g.sem("e2_expert_ps"), g.sem("e2_expert_added")
        GATING = 19
        with nc.Block() as block:
            @block.sync
            def _(sp):
                sp.dma_start(eb[:], g.aps["expert_b"]).then_inc(eb_in, 16)

            @block.tensor
            def _(pe):
                transpose_ops(g, g.X1, ps, xt_ps)
                for t in range(NT):
                    pe.wait_ge(xt_sb, t // 4 + 1)
                    pe.matmul(ps[:, 4, NE * t:NE * t + NE], X1T[:, P * t:P * t + P], g.w("fg"),
                              start=True, stop=True).then_inc(logits, 1)
                pe.wait_ge(xt_sb, NB)
                pe.wait_ge(step, GATING)
                for t in range(NT):
                    pe.transpose(ps[0:NE, t // 4, P * (t % 4):P * (t % 4) + P], comb[:, t, :],
                                 g.k("ident")).then_inc(ct_ps, 1)
                pe.wait_ge(eb_in, 16)
                for t in range(NT):
                    pe.wait_ge(ct_sb, t // 4 + 1)
                    pe.matmul(ps[:, 4 + t // 4, P * (t % 4):P * (t % 4) + P], combT[:, P * t:P * t + P],
                              eb[:], start=True, stop=True).then_inc(bias_ps, 1)
                for t in range(NT):
                    if t == 0:
                        pe.wait_ge(ct_sb, NB)
                    if t == 2:
                        pe.wait_ge(y_start, 1)
                    if t >= 4:
                        pe.wait_ge(e_read, NE * (t - 3))
                    for half in range(2):
                        pe.matmul(ps[:, 2 * (t % 4) + half, :], X1T[:, P * t:P * t + P],
                                  g.w("fe")[:, 512 * half:512 * half + 512],
                                  start=True, stop=True).then_inc(e_ps, 1)

            @block.scalar
            def _(act):
                for b in range(NB):
                    act.wait_ge(xt_ps, 4 * b + 4)
                    nc.scalar.copy(X1T[:, 512 * b:512 * b + 512], ps[:, b, :]).then_inc(xt_sb, 1)
                act.wait_ge(step, 3)
                nc.scalar.activation(gates[:], gates[:], ACT.Exp).then_inc(exps, 1)
                for b in range(NB):
                    act.wait_ge(ct_ps, 4 * b + 4)
                    nc.scalar.copy(combT[:, 512 * b:512 * b + 512], ps[0:NE, b, :]).then_inc(ct_sb, 1)

            @block.vector
            def _(dve):
                n = [0]

                def then(ins):
                    n[0] += 1
                    ins.then_inc(step, 1)
                    dve.wait_ge(step, n[0])

                dve.wait_ge(logits, NT)
                then(dve.tensor_tensor(gates[:], ps[:, 4, 0:NT * NE].rearrange("p (t e) -> p t e", e=NE),
                                       over_tiles(g.r("fgb")), ALU.add))
                then(dve.tensor_reduce(best[:], gates[:], AX_X, ALU.max))
                then(dve.tensor_tensor(gates[:], gates[:], over_cols(best[:], NE), ALU.subtract))
                dve.wait_ge(exps, 1)
                then(dve.tensor_reduce(first[:], gates[:], AX_X, ALU.add))
                then(dve.reciprocal(best[:], first[:]))
                then(dve.tensor_tensor(gates[:], gates[:], over_cols(best[:], NE), ALU.mult))
                left_now = gates
                for i in range(2):
                    then(dve.tensor_reduce(best[:], left_now[:], AX_X, ALU.max))
                    then(dve.tensor_tensor(mark[:], left_now[:], over_cols(best[:], NE), ALU.is_equal))
                    then(dve.tensor_tensor(mark[:], mark[:], over_tiles(g.k("rank")), ALU.mult))
                    then(dve.tensor_reduce(first[:], mark[:], AX_X, ALU.max))
                    if i == 0:
                        then(dve.tensor_tensor(pick[:, 0], mark[:], over_cols(first[:], NE), ALU.is_equal))
                        then(dve.scalar_tensor_tensor(out=left[:], in0=pick[:, 0], scalar=-2.0, in1=gates[:],
                                                      op0=ALU.mult, op1=ALU.add))
                        left_now = left
                then(dve.tensor_tensor(pick[:, 1], mark[:], over_cols(first[:], NE), ALU.is_equal))
                then(dve.tensor_tensor(pick[:, 0], pick[:, 0], pick[:, 1], ALU.add))
                dve.tensor_tensor(comb[:], pick[:, 0], gates[:], ALU.mult).then_inc(step, 1)
                n[0] += 1
                dve.wait_ge(bias_ps, NT)
                dve.wait_ge(step, n[0])
                dve.tensor_tensor(g.Y[:], g.X1[:], ps[:, 4:8, :].rearrange("p b (q e) -> p (b q) e", e=E),
                                  ALU.add).then_inc(y_start, 1)
                dve.wait_ge(y_start, 1)
                for t in range(NT):
                    dve.wait_ge(e_ps, 2 * t + 2)
                    for e in range(NE):
                        if e:
                            dve.wait_ge(e_read, NE * t + e)
                        dve.scalar_tensor_tensor(
                            out=g.Y[:, t, :], in0=ps[:, 2 * (t % 4) + e // 4, P * (e % 4):P * (e % 4) + P],
                            scalar=comb[:, t, e:e + 1], in1=g.Y[:, t, :], op0=ALU.mult,
                            op1=ALU.add).then_inc(e_read, 1)
                assert n[0] == GATING


def add_stage(g, pre, a):
    done = g.sem(pre + "residual")
    with g.nc.Block() as block:
        @block.vector
        def _(dve):
            dve.tensor_tensor(g.Y[:], g.X[:], a[:], ALU.add).then_inc(done, 1)


def rms_transposed(g, ctx, pre, block_engines, src, width, weights, dstT, ps, eps=1e-6):
    nc = g.nc
    G = width // P
    sq = g.sb(ctx, pre + "sq", [P, NT, width])
    ss = g.sb(ctx, pre + "ss", [P, NT])
    squared, summed, rstd, scaled = (g.sem(pre + x) for x in ("squared", "summed", "rstd", "scaled"))
    t_ps, t_sb = g.sem(pre + "t_ps"), g.sem(pre + "t_sb")

    def act(eng):
        nc.scalar.activation(sq[:], src[:], ACT.Square).then_inc(squared, 1)
        for n in range(G):
            for b in range(NB):
                eng.wait_ge(t_ps, 4 * (NB * n + b) + 4)
                nc.scalar.activation(dstT[:, n, 512 * b:512 * b + 512], ps[:, (4 * n + b) % 8, :],
                                     ACT.Identity, scale=g.c(weights, n)).then_inc(t_sb, 1)

    def dve(eng):
        eng.wait_ge(squared, 1)
        eng.tensor_reduce(ss[:], sq[:], AX_X, ALU.add).then_inc(summed, 1)
        eng.wait_ge(summed, 1)
        eng.tensor_scalar(ss[:], ss[:], 1.0 / width, eps, ALU.mult, ALU.add).then_inc(summed, 1)
        for b in range(NB):
            eng.wait_ge(rstd, 1)
            eng.tensor_tensor(sq[:, 4 * b:4 * b + 4, :], src[:, 4 * b:4 * b + 4, :],
                              over_cols(ss[:, 4 * b:4 * b + 4], width), ALU.mult).then_inc(scaled, 1)

    def pool(eng):
        eng.wait_ge(summed, 2)
        eng.tensor_tensor(ss[:], ss[:], g.half[:], ALU.pow).then_inc(rstd, 1)

    def pe(eng):
        for n in range(G):
            for t in range(NT):
                eng.wait_ge(scaled, t // 4 + 1)
                eng.transpose(ps[:, (4 * n + t // 4) % 8, P * (t % 4):P * (t % 4) + P],
                              sq[:, t, P * n:P * n + P], g.k("ident")).then_inc(t_ps, 1)

    return pe, act, dve, pool, t_sb, scaled


def ssm_in_stage(g, m):
    nc = g.nc
    with ExitStack() as ctx:
        UT = g.sb(ctx, "si_UT", [P, 1, S])
        pad = g.sb(ctx, "si_pad", [P, 2, CONV - 1 + S])
        ps = ctx.enter_context(nc.psum_tensor("si_ps", [P, 8, 512], F32))
        rms = ExitStack()
        rpe, ract, rdve, rpool, t_sb, scaled = rms_transposed(g, rms, "si_", None, g.X, E, "mnorm", UT, ps)
        padded, proj, moved, conv = g.sem("si_padded"), g.sem("si_proj"), g.sem("si_moved"), g.sem("si_conv")
        acted = g.sem("si_silu")
        z_ps, z_sb, dt_sb = g.sem("si_z_ps"), g.sem("si_z_sb"), g.sem("si_dt_sb")
        x_ps, x_sb = g.sem("si_x_ps"), g.sem("si_x_sb")
        with nc.Block() as block:
            @block.gpsimd
            def _(pool):
                pool.memset(pad[:, :, 0:CONV - 1], 0.0).then_inc(padded, 1)
                rpool(pool)

            @block.tensor
            def _(pe):
                rpe(pe)
                for n in range(4):
                    if n == 0:
                        pe.wait_ge(t_sb, NB)
                    if n >= 2:
                        pe.wait_ge(moved, n - 1)
                    for b in range(NB):
                        mm = pe.matmul(ps[:, 4 * (n % 2) + b, :], g.w("mxbc")[:, P * n:P * n + P],
                                       UT[:, 0, 512 * b:512 * b + 512], start=True, stop=True)
                    mm.then_inc(proj, 1)
                for t in range(NT):
                    if t == 0:
                        pe.wait_ge(moved, 4)
                    if t >= 8:
                        pe.wait_ge(z_sb, t - 7)
                        pe.wait_ge(dt_sb, t - 7)
                    pe.matmul(ps[:, t % 8, 0:DI + MH], UT[:, 0, P * t:P * t + P], g.w("mzdt"),
                              start=True, stop=True).then_inc(z_ps, 1)
                pe.wait_ge(z_sb, NT)
                pe.wait_ge(dt_sb, NT)
                for n in range(3):
                    pe.wait_ge(acted, n + 1)
                    for t in range(NT):
                        k = NT * n + t
                        if k >= 32 and t % 4 == 0:
                            pe.wait_ge(x_sb, k // 4 - 7)
                        pe.transpose(ps[:, k // 4 % 8, P * (t % 4):P * (t % 4) + P],
                                     m.xbc[:, n, P * t:P * t + P], g.k("ident")).then_inc(x_ps, 1)

            @block.scalar
            def _(act):
                ract(act)
                act.wait_ge(padded, 1)

                def silu(n):
                    act.wait_ge(conv, 4 * n + 4)
                    nc.scalar.activation(m.xbc[:, n, :], m.xbc[:, n, :], ACT.Silu).then_inc(acted, 1)

                for n in range(4):
                    act.wait_ge(proj, n + 1)
                    if n >= 2:
                        act.wait_ge(conv, 4 * (n - 2) + 4)
                    nc.scalar.copy(pad[:, n % 2, CONV - 1:CONV - 1 + S], ps[:, 4 * (n % 2):4 * (n % 2) + 4, :])\
                        .then_inc(moved, 1)
                    if n:
                        silu(n - 1)
                for t in range(NT):
                    act.wait_ge(z_ps, t + 1)
                    nc.scalar.activation(m.z[:, t, :], ps[:, t % 8, 0:DI], ACT.Silu).then_inc(z_sb, 1)
                silu(3)
                for k in range(12):
                    n, b = k // 4, k % 4
                    act.wait_ge(x_ps, 4 * k + 4)
                    src = ps[:, k % 8, :].rearrange("p (q e) -> p q e", e=P)
                    dst = m.xtok[:, 4 * b:4 * b + 4, P * n:P * n + P] if n < 2 else m.btok[:, 4 * b:4 * b + 4, :]
                    nc.scalar.copy(dst, src).then_inc(x_sb, 1)

            @block.vector
            def _(dve):
                rdve(dve)
                for n in range(4):
                    dve.wait_ge(moved, n + 1)
                    dve.tensor_scalar(m.xbc[:, n, :], pad[:, n % 2, CONV - 1:CONV - 1 + S],
                                      g.c("mconv", CONV * n + CONV - 1), g.c("mconvb", n),
                                      ALU.mult, ALU.add).then_inc(conv, 1)
                    for k in range(CONV - 1):
                        dve.wait_ge(conv, 4 * n + k + 1)
                        dve.scalar_tensor_tensor(out=m.xbc[:, n, :], in0=pad[:, n % 2, k:k + S],
                                                 scalar=g.c("mconv", CONV * n + k), in1=m.xbc[:, n, :],
                                                 op0=ALU.mult, op1=ALU.add).then_inc(conv, 1)
                for t in range(NT):
                    dve.wait_ge(z_sb, t + 1)
                    dve.tensor_tensor(m.dt[:, t, :], ps[:, t % 8, DI:DI + MH], g.r("dtb"), ALU.add)\
                       .then_inc(dt_sb, 1)
        rms.close()


def ssm_stage(g, m):
    nc = g.nc
    C = NT
    with ExitStack() as ctx:
        xd = g.sb(ctx, "ss_xd", [P, C, MH, HD])
        xs = m.xs[:].rearrange("p c (h w) -> p c h w", h=MH)
        states = g.sb(ctx, "ss_states", [P, C, DI])
        small = g.sb(ctx, "ss_small", [P, 6, C, MH])
        Aneg = g.sb(ctx, "ss_Aneg", [P, MH])
        a = g.sb(ctx, "ss_a", [P, C, MH])
        decay = g.sb(ctx, "ss_decay", [P, 3, C, MH])
        al = g.sb(ctx, "ss_al", [P, 2, MH, P])
        seg = g.sb(ctx, "ss_seg", [P, 2, MH, P])
        gm = g.sb(ctx, "ss_gm", [P, 2, P])
        carry = g.sb(ctx, "ss_carry", [P, MH, HD])
        xtok = m.xtok[:].rearrange("p c (h w) -> p c h w", h=MH)
        ps = ctx.enter_context(nc.psum_tensor("ss_ps", [P, 8, 512], F32))
        step, lg = g.sem("ss_step"), g.sem("ss_act_step")
        sums_ps, decays = g.sem("ss_sums_ps"), g.sem("ss_decays")
        xs_done, al_done = g.sem("ss_xs_done"), g.sem("ss_al_done")
        d_ps, exp_done = g.sem("ss_d_ps"), g.sem("ss_exp_done")
        gm_done, w_done = g.sem("ss_gm_done"), g.sem("ss_w_done")
        dh_ps, h_step, y_ps, y_step = g.sem("ss_dh_ps"), g.sem("ss_h_step"), g.sem("ss_y_ps"), g.sem("ss_y_step")
        skip = g.sem("ss_skip")
        CB, CT = 2, 3
        DT_STEPS = 4
        with nc.Block() as block:
            @block.gpsimd
            def _(pool):
                for c in range(C):
                    if c == 0:
                        pool.wait_ge(step, 10)
                    if c >= 2:
                        pool.wait_ge(d_ps, c - 1)
                    pool.tensor_tensor(al[:, c % 2], g.k("upto").unsqueeze(1).to_broadcast([P, MH, P]),
                                       over_cols(a[:, c, :], P), ALU.mult).then_inc(al_done, 1)

            @block.tensor
            def _(pe):
                pe.wait_ge(step, 10)
                for n, name in enumerate(("upto", "after", "ones")):
                    mm = pe.matmul(ps[:, 7, C * MH * n:C * MH * (n + 1)], g.k(name),
                                   a[:].rearrange("p c h -> p (c h)"), start=True, stop=True)
                mm.then_inc(sums_ps, 1)

                def first(c):
                    if c >= 2:
                        pe.wait_ge(exp_done, c - 1)
                        pe.wait_ge(gm_done, c - 1)
                    pe.matmul(ps[:, 2 + c % 2, 0:P], m.xbc[:, CB, P * c:P * c + P],
                              m.xbc[:, CT, P * c:P * c + P], start=True, stop=True)
                    pe.wait_ge(al_done, c + 1)
                    pe.matmul(ps[:, c % 2, :], g.k("after"), al[:, c % 2].rearrange("p h i -> p (h i)"),
                              start=True, stop=True).then_inc(d_ps, 1)

                def state(c):
                    pe.wait_ge(xs_done, 2)
                    if c >= 2:
                        pe.wait_ge(h_step, 2 * c - 1)
                    pe.matmul(ps[:, 4 + c % 2, 0:DI], m.btok[:, c, :], m.xs[:, c, :],
                              start=True, stop=True).then_inc(dh_ps, 1)

                def outputs(c):
                    if c >= 1:
                        pe.wait_ge(y_step, DT_STEPS + 3 * (c - 1) + 2)
                    pe.wait_ge(w_done, c + 1)
                    for h in range(MH):
                        pe.matmul(ps[:, 6, HD * h:HD * h + HD], seg[:, c % 2, h, :], xd[:, c, h, :],
                                  start=True, stop=True)
                    pe.wait_ge(h_step, 2 * c + 1)
                    pe.matmul(ps[:, 6, DI:2 * DI], m.xbc[:, CT, P * c:P * c + P], states[:, c, :],
                              start=True, stop=True).then_inc(y_ps, 1)

                first(0)
                for c in range(C):
                    if c + 1 < C:
                        first(c + 1)
                    if c + 1 < C:
                        state(c)
                    outputs(c)

            @block.scalar
            def _(act):
                nc.scalar.activation(Aneg[:], g.r("alog"), ACT.Exp).then_inc(lg, 1)
                act.wait_ge(step, 1)
                nc.scalar.activation(small[:, 0], small[:, 0], ACT.Exp).then_inc(lg, 1)
                act.wait_ge(step, 2)
                nc.scalar.activation(small[:, 2], small[:, 1], ACT.Ln).then_inc(lg, 1)
                act.wait_ge(sums_ps, 1)
                nc.scalar.activation(decay[:].rearrange("p n c h -> p (n c h)"), ps[:, 7, 0:3 * C * MH],
                                     ACT.Exp).then_inc(decays, 1)
                for c in range(C):
                    act.wait_ge(d_ps, c + 1)
                    if c >= 2:
                        act.wait_ge(y_ps, c - 1)
                    nc.scalar.activation(seg[:, c % 2].rearrange("p h i -> p (h i)"), ps[:, c % 2, :],
                                         ACT.Exp).then_inc(exp_done, 1)

            @block.vector
            def _(dve):
                n = [0]

                def then(ins):
                    n[0] += 1
                    ins.then_inc(step, 1)
                    dve.wait_ge(step, n[0])

                raw, one_more, log, gap = small[:, 0], small[:, 1], small[:, 2], small[:, 3]
                dve.tensor_scalar(small[:, 5], m.dt[:], -1.0, None, ALU.mult).then_inc(y_step, 1)
                dve.wait_ge(y_step, 1)
                then(dve.tensor_tensor(raw, m.dt[:], small[:, 5], ALU.min))
                dve.wait_ge(lg, 2)
                then(dve.tensor_scalar(one_more, raw, 1.0, None, ALU.add))
                then(dve.tensor_scalar(gap, one_more, -1.0, None, ALU.add))
                then(dve.tensor_scalar(small[:, 4], gap, 0.0, None, ALU.is_equal))
                then(dve.tensor_tensor(gap, gap, small[:, 4], ALU.add))
                then(dve.reciprocal(small[:, 5], gap))
                dve.wait_ge(lg, 3)
                then(dve.tensor_tensor(log, log, small[:, 5], ALU.mult))
                then(dve.tensor_tensor(log, log, small[:, 4], ALU.add))
                then(dve.tensor_tensor(log, log, raw, ALU.mult))
                dve.tensor_scalar(m.dt[:], m.dt[:], 0.0, None, ALU.max).then_inc(y_step, 1)
                dve.wait_ge(y_step, 2)
                dve.tensor_tensor(m.dt[:], m.dt[:], log, ALU.add).then_inc(y_step, 1)
                dve.wait_ge(y_step, 3)
                dve.tensor_scalar(gap, m.dt[:], -1.0, None, ALU.mult).then_inc(y_step, 1)
                dve.wait_ge(y_step, 4)
                then(dve.tensor_tensor(a[:], gap, over_tiles(Aneg[:], C), ALU.mult))
                tok = lambda v: v.rearrange("p c h w -> p (c h) w")
                dtv = m.dt[:].rearrange("p c h -> p (c h)")
                dve.tensor_tensor(tok(xd[:]), tok(xtok), over_cols(dtv, HD), ALU.mult).then_inc(xs_done, 1)
                dve.wait_ge(xs_done, 1)
                dve.wait_ge(decays, 1)
                dve.tensor_tensor(tok(xs), tok(xd[:]),
                                  over_cols(decay[:, 1].rearrange("p c h -> p (c h)"), HD), ALU.mult)\
                   .then_inc(xs_done, 1)
                dskip = g.r("dskip").unsqueeze(1).to_broadcast([P, C, MH]).unsqueeze(3)\
                    .to_broadcast([P, C, MH, HD])
                dve.tensor_tensor(xtok, xtok, dskip, ALU.mult).then_inc(skip, 1)
                dve.memset(states[:, 0, :], 0.0).then_inc(h_step, 1)
                for c in range(C):
                    dve.wait_ge(d_ps, c + 1)
                    if c >= 2:
                        dve.wait_ge(w_done, c - 1)
                    dve.tensor_tensor(gm[:, c % 2], ps[:, 2 + c % 2, 0:P], g.k("upto"), ALU.mult)\
                       .then_inc(gm_done, 1)
                    dve.wait_ge(gm_done, c + 1)
                    dve.wait_ge(exp_done, c + 1)
                    dve.tensor_tensor(seg[:, c % 2], seg[:, c % 2],
                                      gm[:, c % 2].unsqueeze(1).to_broadcast([P, MH, P]), ALU.mult)\
                       .then_inc(w_done, 1)
                    if c + 1 < C:
                        dve.wait_ge(h_step, 2 * c + 1)
                        dve.tensor_tensor(carry[:], states[:, c, :].rearrange("p (h w) -> p h w", h=MH),
                                          over_cols(decay[:, 2, c, :], HD), ALU.mult).then_inc(h_step, 1)
                        dve.wait_ge(h_step, 2 * c + 2)
                        dve.wait_ge(dh_ps, c + 1)
                        dve.tensor_tensor(states[:, c + 1, :], carry[:].rearrange("p h w -> p (h w)"),
                                          ps[:, 4 + c % 2, 0:DI], ALU.add).then_inc(h_step, 1)
                    dve.wait_ge(y_ps, c + 1)
                    dve.wait_ge(dh_ps, min(c + 1, C - 1))
                    dve.tensor_tensor(xs[:, c], ps[:, 6, DI:2 * DI].rearrange("p (h w) -> p h w", h=MH),
                                      over_cols(decay[:, 0, c, :], HD), ALU.mult).then_inc(y_step, 1)
                    dve.wait_ge(y_step, DT_STEPS + 3 * c + 1)
                    dve.tensor_tensor(m.xs[:, c, :], m.xs[:, c, :], ps[:, 6, 0:DI], ALU.add).then_inc(y_step, 1)
                    dve.wait_ge(y_step, DT_STEPS + 3 * c + 2)
                    if c == 0:
                        dve.wait_ge(skip, 1)
                    dve.tensor_tensor(m.xs[:, c, :], m.xs[:, c, :], m.xtok[:, c, :], ALU.add)\
                       .then_inc(y_step, 1)
                dve.wait_ge(y_step, DT_STEPS + 3 * C)
                dve.tensor_tensor(m.xs[:], m.xs[:], m.z[:], ALU.mult).then_inc(skip, 1)


def ssm_out_stage(g, m):
    nc = g.nc
    with ExitStack() as ctx:
        YT = g.sb(ctx, "so_YT", [P, 2, S])
        ps = ctx.enter_context(nc.psum_tensor("so_ps", [P, 8, 512], F32))
        rpe, ract, rdve, rpool, t_sb, scaled = rms_transposed(g, ctx, "so_", None, m.xs, DI, "mssm", YT, ps)
        o_ps, done = g.sem("so_o_ps"), g.sem("so_done")
        with nc.Block() as block:
            @block.gpsimd
            def _(pool):
                rpool(pool)

            @block.scalar
            def _(act):
                ract(act)

            @block.tensor
            def _(pe):
                rpe(pe)
                pe.wait_ge(t_sb, 2 * NB)
                for t in range(NT):
                    for n in range(2):
                        mm = pe.matmul(ps[:, t // 4, P * (t % 4):P * (t % 4) + P], YT[:, n, P * t:P * t + P],
                                       g.w("mo")[:, E * n:E * n + E], start=(n == 0), stop=(n == 1))
                    mm.then_inc(o_ps, 1)

            @block.vector
            def _(dve):
                rdve(dve)
                dve.wait_ge(o_ps, NT)
                dve.tensor_tensor(g.Y[:], g.X[:], ps[:, 0:4, :].rearrange("p b (q e) -> p (b q) e", e=E),
                                  ALU.add).then_inc(done, 1)


def mlp_stage(g):
    nc = g.nc
    rows = [min(P, INTER - P * n) for n in range(3)]
    with ExitStack() as ctx:
        NTt = g.sb(ctx, "ml_NT", [P, 1, S])
        hid = g.sb(ctx, "ml_hid", [P, 3, S])
        ps = ctx.enter_context(nc.psum_tensor("ml_ps", [P, 8, 512], F32))
        rpe, ract, rdve, rpool, t_sb, scaled = rms_transposed(g, ctx, "ml_", None, g.Y, E, "mpost", NTt, ps)
        gate_ps, up_ps, acted, hid_done = (g.sem("ml_" + x) for x in ("gate_ps", "up_ps", "acted", "hid_done"))
        d_ps, res, done = g.sem("ml_down_ps"), g.sem("ml_res"), g.sem("ml_done")
        steps = [(n, b) for n in range(3) for b in range(NB)]
        with nc.Block() as block:
            @block.sync
            def _(sp):
                sp.dma_start(g.XW[:], g.aps["experts"]).then_inc(g.experts_in, 16)
                sp.dma_start(g.sel[:], g.aps["select"]).then_inc(g.experts_in, 16)

            @block.gpsimd
            def _(pool):
                rpool(pool)

            @block.scalar
            def _(act):
                ract(act)
                for i, (n, b) in enumerate(steps):
                    r = rows[n]
                    act.wait_ge(gate_ps, i + 1)
                    nc.scalar.activation(hid[0:r, n, 512 * b:512 * b + 512], ps[0:r, 2 * (i % 4), :],
                                         ACT.Silu).then_inc(acted, 1)

            @block.tensor
            def _(pe):
                rpe(pe)
                pe.wait_ge(t_sb, NB)
                for i, (n, b) in enumerate(steps):
                    r = rows[n]
                    if i >= 4:
                        pe.wait_ge(hid_done, i - 3)
                    pe.matmul(ps[0:r, 2 * (i % 4), :], g.w("mg")[:, P * n:P * n + r],
                              NTt[:, 0, 512 * b:512 * b + 512], start=True, stop=True).then_inc(gate_ps, 1)
                    pe.matmul(ps[0:r, 2 * (i % 4) + 1, :], g.w("mu")[:, P * n:P * n + r],
                              NTt[:, 0, 512 * b:512 * b + 512], start=True, stop=True).then_inc(up_ps, 1)
                pe.wait_ge(hid_done, len(steps))
                for t in range(NT):
                    for n in range(3):
                        r = rows[n]
                        mm = pe.matmul(ps[:, t // 4, P * (t % 4):P * (t % 4) + P], hid[0:r, n, P * t:P * t + P],
                                       g.w("md")[0:r, E * n:E * n + E], start=(n == 0), stop=(n == 2))
                    mm.then_inc(d_ps, 1)

            @block.vector
            def _(dve):
                rdve(dve)
                dve.wait_ge(scaled, NB)
                dve.tensor_tensor(g.Y[:], g.Y[:], g.X[:], ALU.add).then_inc(res, 1)
                for i, (n, b) in enumerate(steps):
                    r = rows[n]
                    dve.wait_ge(up_ps, i + 1)
                    dve.wait_ge(acted, i + 1)
                    h = hid[0:r, n, 512 * b:512 * b + 512]
                    dve.tensor_tensor(h, h, ps[0:r, 2 * (i % 4) + 1, :], ALU.mult).then_inc(hid_done, 1)
                dve.wait_ge(d_ps, NT)
                dve.wait_ge(res, 1)
                dve.tensor_tensor(g.Y[:], g.Y[:], ps[:, 0:4, :].rearrange("p b (q e) -> p (b q) e", e=E),
                                  ALU.add).then_inc(done, 1)


def experts8_stage(g):
    nc = g.nc
    xw = lambda name, e: g.XW[:, X_COLS[name][0] + E * e:X_COLS[name][0] + E * e + E]
    NX = RE + 1
    with ExitStack() as ctx:
        XT = g.sb(ctx, "e8_XT", [P, S])
        YT = g.sb(ctx, "e8_YT", [P, S])
        score = g.sb(ctx, "e8_score", [P, NT, RE])
        ranked = g.sb(ctx, "e8_ranked", [P, NT, RE])
        left = g.sb(ctx, "e8_left", [P, NT, RE])
        top = g.sb(ctx, "e8_top", [P, NT, TOPK])
        total = g.sb(ctx, "e8_total", [P, NT])
        rest = g.sb(ctx, "e8_rest", [RE, S])
        cparts = g.sb(ctx, "e8_cparts", [96, S], BF16)
        sel = g.sb(ctx, "e8_sel", [96, RE * P], BF16)
        hid = g.sb(ctx, "e8_hid", [P, 2, 512])
        prod = g.sb(ctx, "e8_prod", [P, 2, 512])
        ps = ctx.enter_context(nc.psum_tensor("e8_ps", [P, 8, 512], F32))
        xt_ps, xt_sb, logits, sig = g.sem("e8_xt_ps"), g.sem("e8_xt_sb"), g.sem("e8_logits"), g.sem("e8_sig")
        step, ct_ps = g.sem("e8_step"), g.sem("e8_ct_ps")
        zeroed, c_done = g.sem("e8_zeroed"), g.sem("e8_c_done")
        gu_ps, c_ps, acted, used = g.sem("e8_gu_ps"), g.sem("e8_c_ps"), g.sem("e8_acted"), g.sem("e8_used")
        h_done, down, out_sb = g.sem("e8_h_done"), g.sem("e8_down"), g.sem("e8_out_sb")
        back, done = g.sem("e8_back"), g.sem("e8_done")
        CHOICE = 1 + 2 * NT + 6
        with nc.Block() as block:
            @block.gpsimd
            def _(pool):
                pool.memset(cparts[:], 0.0).then_inc(zeroed, 1)
                pool.wait_ge(zeroed, 1)
                pool.wait_ge(g.experts_in, 32)
                pool.tensor_copy(sel[:], g.sel[:]).then_inc(zeroed, 1)

            @block.tensor
            def _(pe):
                transpose_ops(g, g.X, ps, xt_ps)
                for t in range(NT):
                    pe.wait_ge(xt_sb, t // 4 + 1)
                    pe.matmul(ps[:, 4, RE * t:RE * t + RE], XT[:, P * t:P * t + P], g.w("rg"),
                              start=True, stop=True).then_inc(logits, 1)
                pe.wait_ge(xt_sb, NB)
                pe.wait_ge(step, CHOICE)
                for t in range(NT):
                    pe.transpose(ps[0:RE, t // 4, P * (t % 4):P * (t % 4) + P], score[:, t, :],
                                 g.k("ident")).then_inc(ct_ps, 1)
                pe.wait_ge(c_done, 5)
                pe.wait_ge(g.experts_in, 32)
                pe.wait_ge(zeroed, 2)

                pe.nop().then_inc(h_done, 2)
                with pe.Fori(0, NB) as b:
                    tok = bass.ds(512 * b, 512)
                    for e in range(NX + 1):
                        if e < NX:
                            pe.wait_ge(h_done, NX * b + (e + 1 if e >= 2 else 2))
                            pe.matmul(ps[:, e % 2, :], xw("gate", e), XT[:, tok], start=True, stop=True)\
                                .then_inc(gu_ps, 1)
                            pe.matmul(ps[:, 2 + e % 2, :], xw("up", e), XT[:, tok], start=True, stop=True)\
                                .then_inc(gu_ps, 1)
                            if e < RE:
                                pe.matmul(ps[:, 4 + e % 2, :], sel[:, P * e:P * e + P], cparts[:, tok],
                                          start=True, stop=True).then_inc(c_ps, 1)
                        if e:
                            d = e - 1
                            pe.wait_ge(h_done, NX * b + d + 3)
                            if d == 0:
                                pe.wait_ge(out_sb, b + 1)
                            pe.matmul(ps[:, 7, :], xw("down", d), hid[:, d % 2, :], start=(d == 0),
                                      stop=(d == NX - 1)).then_inc(down, 1)
                pe.wait_ge(out_sb, NB + 1)
                for t in range(NT):
                    pe.transpose(ps[:, t // 4, P * (t % 4):P * (t % 4) + P], YT[:, P * t:P * t + P],
                                 g.k("ident")).then_inc(back, 1)

            @block.scalar
            def _(act):
                for b in range(NB):
                    act.wait_ge(xt_ps, 4 * b + 4)
                    nc.scalar.copy(XT[:, 512 * b:512 * b + 512], ps[:, b, :]).then_inc(xt_sb, 1)
                act.wait_ge(logits, NT)
                nc.scalar.activation(score[:].rearrange("p t e -> p (t e)"), ps[:, 4, 0:NT * RE],
                                     ACT.Sigmoid).then_inc(sig, 1)
                act.nop().then_inc(down, 2)
                act.nop().then_inc(out_sb, 1)
                with act.Fori(0, NB) as b:
                    for e in range(NX):
                        act.wait_ge(gu_ps, 2 * NX * b + 2 * e + 1)
                        act.wait_ge(h_done, NX * b + max(e + 1, 2))
                        nc.scalar.activation(prod[:, e % 2, :], ps[:, e % 2, :], ACT.Silu).then_inc(acted, 1)
                    act.wait_ge(down, NX * b + NX + 2)
                    nc.scalar.copy(YT[:, bass.ds(512 * b, 512)], ps[:, 7, :]).then_inc(out_sb, 1)

            @block.vector
            def _(dve):
                n = [0]

                def then(ins):
                    n[0] += 1
                    ins.then_inc(step, 1)
                    dve.wait_ge(step, n[0])

                dve.wait_ge(sig, 1)
                then(dve.tensor_tensor(ranked[:], score[:], over_tiles(g.r("ebias")), ALU.add))
                for t in range(NT):
                    dve.max(top[:, t, :], ranked[:, t, :]).then_inc(step, 1)
                    n[0] += 1
                dve.wait_ge(step, n[0])
                for t in range(NT):
                    dve.match_replace(left[:, t, :], top[:, t, :], ranked[:, t, :], NEG).then_inc(step, 1)
                    n[0] += 1
                dve.wait_ge(step, n[0])
                then(dve.tensor_tensor(ranked[:], ranked[:], left[:], ALU.not_equal))
                then(dve.tensor_tensor(score[:], score[:], ranked[:], ALU.mult))
                then(dve.tensor_reduce(total[:], score[:], AX_X, ALU.add))
                then(dve.reciprocal(total[:], total[:]))
                then(dve.tensor_scalar(total[:], total[:], ROUTE_SCALE, None, ALU.mult))
                then(dve.tensor_tensor(score[:], score[:], over_cols(total[:], RE), ALU.mult))
                dve.wait_ge(ct_ps, NT)
                dve.wait_ge(zeroed, 1)
                turned = ps[0:RE, 0:4, :]
                four = lambda v: v.rearrange("p (b t) -> p b t", t=512)
                dve.tensor_copy(four(cparts[0:RE, :]), turned).then_inc(c_done, 1)
                dve.wait_ge(c_done, 1)
                dve.tensor_tensor(four(rest[:]), turned, four(cparts[0:RE, :]), ALU.subtract).then_inc(c_done, 1)
                dve.wait_ge(c_done, 2)
                dve.tensor_copy(cparts[32:32 + RE, :], rest[:]).then_inc(c_done, 1)
                dve.wait_ge(c_done, 3)
                dve.tensor_tensor(rest[:], rest[:], cparts[32:32 + RE, :], ALU.subtract).then_inc(c_done, 1)
                dve.wait_ge(c_done, 4)
                dve.tensor_copy(cparts[64:64 + RE, :], rest[:]).then_inc(c_done, 1)
                with dve.Fori(0, NB) as b:
                    for e in range(NX):
                        dve.wait_ge(gu_ps, 2 * NX * b + 2 * e + 2)
                        dve.wait_ge(acted, NX * b + e + 1)
                        dve.wait_ge(down, NX * b + max(e + 1, 2))
                        h, p = hid[:, e % 2, :], prod[:, e % 2, :]
                        if e < RE:
                            dve.tensor_tensor(p, p, ps[:, 2 + e % 2, :], ALU.mult).then_inc(used, 1)
                            dve.wait_ge(used, RE * b + e + 1)
                            dve.wait_ge(c_ps, RE * b + e + 1)
                            dve.tensor_tensor(h, p, ps[:, 4 + e % 2, :], ALU.mult).then_inc(h_done, 1)
                        else:
                            dve.tensor_tensor(h, p, ps[:, 2 + e % 2, :], ALU.mult).then_inc(h_done, 1)
                dve.wait_ge(back, NT)
                dve.tensor_tensor(g.Y[:], g.X[:], ps[:, 0:4, :].rearrange("p b (q e) -> p (b q) e", e=E),
                                  ALU.add).then_inc(done, 1)


class Mamba:
    pass


STOP = None


def layers(nc, aps, out):
    with ExitStack() as ctx:
        g = Core(nc)
        g.aps = aps
        g.X = g.sb(ctx, "X", [P, NT, E])
        g.Y = g.sb(ctx, "Y", [P, NT, E])
        g.W = g.sb(ctx, "W", [P, W_N])
        g.C = g.sb(ctx, "C", [P, C_N])
        g.R = g.sb(ctx, "R", [P, R_N])
        g.K = g.sb(ctx, "K", [P, K_N])
        g.identb = g.sb(ctx, "identb", [P, P], BF16)
        g.mask_qk = g.sb(ctx, "mask_qk", [P, P], BF16)
        g.mask_kq = g.sb(ctx, "mask_kq", [P, P], BF16)
        g.half = g.sb(ctx, "minus_half", [P, NT])
        load_stage(g, aps)

        def attention(pre, causal, *names):
            with ExitStack() as actx:
                g.V = g.sb(actx, pre + "V", [P, NT, E])
                project_stage(g, pre, *names[:6], rope=causal)
                if STOP == pre + "proj":
                    return
                g.OT = g.sb(actx, pre + "OT", [P, NG, S])
                attention_stage(g, pre, causal)
                if STOP == pre + "attn":
                    return
                attention_out_stage(g, pre, *names[6:])
                if not causal:
                    return norm_stage(g, pre + "n")
                g.X1 = g.sb(actx, "X1", [P, NT, E])
                norm_stage(g, pre + "n", 1e-5, "ln1w", "ln1b", out=g.X1)
                experts2_stage(g)
                norm_stage(g, "e2n", 1e-5, "ln2w", "ln2b", out=g.X1)
                add_stage(g, "l2_", g.X1)
                norm_stage(g, "l2n")

        def finish(src=None):
            out_sent = g.sem("out_sent")
            with nc.Block() as block:
                @block.sync
                def _(sp):
                    sp.dma_start(out.rearrange("o (t p) e -> p (o t) e", p=P), (src or g.X)[:]).then_inc(out_sent, 16)
                    sp.wait_ge(out_sent, 16)

        attention("a_", False, "wq", "wk", "wv", "bq", "bk", "bv", "wo", "bo")
        if STOP and STOP.startswith("a_"):
            return finish()
        attention("f_", True, "fq", "fk", "fv", "fbq", "fbk", "fbv", "fo", "fbo")
        if STOP and STOP.startswith("f_"):
            return finish()
        g.recycle()
        with ExitStack() as mctx:
            m = Mamba()
            m.dt = g.sb(mctx, "m_dt", [P, NT, MH])
            m.xbc = g.sb(mctx, "m_xbc", [P, 4, S])
            m.z = g.sb(mctx, "m_z", [P, NT, DI])
            m.xtok = g.sb(mctx, "m_xtok", [P, NT, DI])
            m.btok = g.sb(mctx, "m_btok", [P, NT, NS])
            ssm_in_stage(g, m)
            m.xs = g.sb(mctx, "m_xs", [P, NT, DI])
            ssm_stage(g, m)
            ssm_out_stage(g, m)
            if STOP == "m_":
                return finish(g.Y)
        with ExitStack() as xctx:
            g.XW = g.sb(xctx, "experts_w", [P, X_N])
            g.sel = g.sb(xctx, "select", [96, RE * P])
            g.experts_in = g.sem("experts_in")
            mlp_stage(g)
            norm_stage(g, "m_n")
            if STOP == "n_":
                return finish()
            experts8_stage(g)
            norm_stage(g, "x_n")
        return finish()


def host_layout(inputs):
    f = {k: np.asarray(v) for k, v in inputs.items()}
    a, m, r = "L0_attn_", "L1_attn_", "L1_ffn_"
    fw = f["L0_ffn_in_proj_w"]
    mw = f[m + "in_proj_w"]
    down = np.zeros((3 * P, E), np.float32)
    down[:INTER] = f[m + "down_w"].T
    parts = {
        "wq": f[a + "Wq"], "wk": f[a + "Wk"], "wv": f[a + "Wv"], "wo": f[a + "Wo"],
        "fq": fw[0:E].T, "fk": fw[E:2 * E].T, "fv": fw[2 * E:].T, "fo": f["L0_ffn_out_proj_w"].T,
        "fg": f["L0_ffn_gate_w"].T, "fe": f["L0_ffn_expert_w"].transpose(2, 0, 1).reshape(E, NE * E),
        "mxbc": mw[DI:2 * DI + 2 * NS].T, "mzdt": np.concatenate([mw[0:DI], mw[2 * DI + 2 * NS:]]).T,
        "mo": f[m + "out_proj_w"].T.reshape(2, P, E).transpose(1, 0, 2).reshape(P, 2 * E),
        "mg": f[m + "gate_w"].T, "mu": f[m + "up_w"].T,
        "md": down.reshape(3, P, E).transpose(1, 0, 2).reshape(P, 3 * E), "rg": f[r + "gate_w"].T,
    }
    weights = np.ascontiguousarray(np.concatenate([parts[n] for n in W_COLS], axis=1))
    fb = f["L0_ffn_in_proj_b"]
    cols = {
        "bq": f[a + "bq"][:, None], "bk": f[a + "bk"][:, None], "fbq": fb[0:E][:, None],
        "fbk": fb[E:2 * E][:, None], "mnorm": f[m + "norm_w"][:, None],
        "mconv": f[m + "conv_w"].reshape(4, P, CONV).transpose(1, 0, 2).reshape(P, 4 * CONV),
        "mconvb": f[m + "conv_b"].reshape(4, P).T, "mssm": f[m + "ssm_norm_w"].reshape(2, P).T,
        "mpost": f[m + "post_norm_w"][:, None],
    }
    rows = {
        "bv": f[a + "bv"], "bo": f[a + "bo"], "fbv": fb[2 * E:], "fbo": f["L0_ffn_out_proj_b"],
        "ln1w": f["L0_ffn_ln1_w"], "ln1b": f["L0_ffn_ln1_b"], "ln2w": f["L0_ffn_ln2_w"],
        "ln2b": f["L0_ffn_ln2_b"], "fgb": f["L0_ffn_gate_b"], "dtb": f[m + "dt_bias"],
        "alog": f[m + "A_log"], "dskip": f[m + "D"], "ebias": f[r + "expert_bias"],
    }
    stack = lambda e, s, order: np.concatenate([f[r + e], f[r + s][None]]).transpose(order).reshape(P, -1)
    experts = {
        "gate": stack("w_gate", "shared_gate_w", (2, 0, 1)), "up": stack("w_up", "shared_up_w", (2, 0, 1)),
        "down": stack("w_down", "shared_down_w", (2, 0, 1)),
    }
    i = np.arange(P)
    consts = {
        "ident": np.eye(P), "mask_qk": np.where(i[None, :] > i[:, None], NEG, 0.0),
        "mask_kq": np.where(i[:, None] > i[None, :], NEG, 0.0),
        "upto": i[:, None] <= i[None, :], "after": i[:, None] > i[None, :], "ones": np.ones((P, P)),
        "rank": np.tile(np.arange(NE, 0, -1), (P, 1)),
    }
    inv = (1.0 / 10000.0 ** (np.arange(0, D, 2, dtype=np.float32) / D)).astype(np.float32)
    angle = (np.arange(S, dtype=np.float32)[:, None] * inv[None, :]).astype(np.float32).astype(np.float64)
    cos = np.repeat(np.tile(np.cos(angle), (1, H)), 2, axis=1)
    sin = np.repeat(np.tile(np.sin(angle), (1, H)), 2, axis=1)
    sin[:, 0::2] *= -1.0
    c32 = lambda x: np.ascontiguousarray(x, dtype=np.float32)
    return {
        "x": np.ascontiguousarray(f[a + "inputs"].reshape(S, E)),
        "weights": weights, "cols": np.concatenate([cols[n] for n in C_COLS], axis=1),
        "rows": np.concatenate([rows[n] for n in R_COLS]),
        "experts": np.ascontiguousarray(np.concatenate([experts[n] for n in X_COLS], axis=1)),
        "expert_b": f["L0_ffn_expert_b"],
        "consts": c32(np.concatenate([consts[n] for n in K_COLS], axis=1)),
        "rope_cos": c32(cos), "rope_sin": c32(sin),
        "select": np.repeat(np.tile(np.eye(32, RE), (3, 1)), P, axis=1).astype(np.float32),
    }


def kernel(**inputs):
    import concourse.bacc as bacc
    from concourse.bass_utils import run_bass_kernel_spmd

    nc = bacc.Bacc("TRN2", target_bir_lowering=False, num_devices=1)
    arrays = {f"in_{n}": a for n, a in host_layout(inputs).items()}
    aps = {n[3:]: nc.dram_tensor(n, a.shape, mybir.dt.from_np(a.dtype), kind="ExternalInput").ap()
           for n, a in arrays.items()}
    out = nc.dram_tensor("out", (1, S, E), F32, kind="ExternalOutput").ap()
    layers(nc, aps, out)
    result = run_bass_kernel_spmd(nc, [arrays], core_ids=[0])
    return result.results[0]["out"]
```
